# Optimizing a Trainium2 kernel written in Bass

```python
import numpy as np
import jax
import jax.numpy as jnp

def _softmax(x, axis=-1):
    return jax.nn.softmax(x, axis=axis)

def _gelu(x):
    return jax.nn.gelu(x, approximate=True)

def _silu(x):
    return jax.nn.silu(x)

def _sigmoid(x):
    return jax.nn.sigmoid(x)

def _layernorm(x, axis=-1, eps=1e-05):
    m = jnp.mean(x, axis=axis, keepdims=True)
    v = jnp.var(x, axis=axis, keepdims=True)
    return (x - m) / jnp.sqrt(v + eps)

def _scatter_add(tgt, idx, src, axis=0):
    return tgt.at[idx].add(src)

def _segment_sum(src, seg, n):
    return jax.ops.segment_sum(src, seg, n)
kernel_name = 'mk_gnn_resnorm_d1_gnn_r8_3713f8'

def setup_inputs(seed: int=0):
    np.random.seed(seed)
    _w = jnp.asarray

    def _rec_inputs():
        import jax
        import jax.numpy as jnp
        _gk = jax.random.key(seed)
        x = -0.000202 + 1 * jax.random.normal(jax.random.fold_in(_gk, 1), (6250, 128), jnp.float32)
        src = jax.random.randint(jax.random.fold_in(_gk, 2), (200000,), 0, 6250, jnp.int32)
        dst = jnp.minimum((6250 * jax.random.uniform(jax.random.fold_in(_gk, 3), (200000,)) ** 2.0).astype(jnp.int32), 49999)
        _o = jnp.argsort(dst, stable=True)
        src = src[_o]
        dst = dst[_o]
        edge_attr_64 = -7.08334e-05 + 0.999895 * jax.random.normal(jax.random.fold_in(_gk, 11), (200000, 64), jnp.float32)
        return (x, src, dst, edge_attr_64)
    x, src, dst, edge_attr_64 = _rec_inputs()

    def _L0_gnn_setup():
        import jax, jax.numpy as jnp
        import numpy as np
        N = 6250
        E = 75000
        HID = 128
        EDIM = 64
        BN_EPS = 1e-05
        key = jax.random.key(seed)
        ks = jax.random.split(key, 10)
        s = 1.0 / np.sqrt(HID)
        se = 1.0 / np.sqrt(EDIM)
        return {'x': jax.random.normal(ks[0], (N, HID), jnp.float32), 'edge_attr': jax.random.normal(ks[1], (E, EDIM), jnp.float32), 'We': jax.random.uniform(ks[2], (EDIM, HID), jnp.float32, -se, se), 'be': jnp.zeros((HID,), jnp.float32), 'W1': jax.random.uniform(ks[3], (HID, HID), jnp.float32, -s, s), 'b1': jnp.zeros((HID,), jnp.float32), 'W2': jax.random.uniform(ks[4], (HID, HID), jnp.float32, -s, s), 'b2': jnp.zeros((HID,), jnp.float32), 'gamma': jnp.ones((HID,), jnp.float32), 'beta': jnp.zeros((HID,), jnp.float32), 'eps': jnp.zeros((), jnp.float32), 'edge_index': jax.random.randint(ks[5], (2, E), 0, N, jnp.int32)}
    _L0_gnn_all = _L0_gnn_setup()
    _L0_gnn_in = {k: v for k, v in _L0_gnn_all.items() if k in ('We', 'be', 'W1', 'b1', 'W2', 'b2', 'gamma', 'beta', 'eps')}
    del _L0_gnn_all
    return {'x': x, 'src': src, 'dst': dst, 'edge_attr_64': edge_attr_64, 'L0_gnn_We': _L0_gnn_in['We'], 'L0_gnn_be': _L0_gnn_in['be'], 'L0_gnn_W1': _L0_gnn_in['W1'], 'L0_gnn_b1': _L0_gnn_in['b1'], 'L0_gnn_W2': _L0_gnn_in['W2'], 'L0_gnn_b2': _L0_gnn_in['b2'], 'L0_gnn_gamma': _L0_gnn_in['gamma'], 'L0_gnn_beta': _L0_gnn_in['beta'], 'L0_gnn_eps': _L0_gnn_in['eps']}

def reference(x, src, dst, edge_attr_64, L0_gnn_We, L0_gnn_be, L0_gnn_W1, L0_gnn_b1, L0_gnn_W2, L0_gnn_b2, L0_gnn_gamma, L0_gnn_beta, L0_gnn_eps):
    import jax
    import jax.numpy as jnp

    def _L0_gnn_ref(x, edge_attr, We, be, W1, b1, W2, b2, gamma, beta, eps, edge_index):
        import jax, jax.numpy as jnp
        import numpy as np
        N = 6250
        E = 75000
        HID = 128
        EDIM = 64
        BN_EPS = 1e-05
        src, dst = (edge_index[0], edge_index[1])
        msg = jax.nn.relu(x[src] + edge_attr @ We + be)
        aggr = jax.ops.segment_sum(msg, dst, num_segments=N)
        h = (1.0 + eps) * x + aggr
        h = jax.nn.relu(h @ W1 + b1) @ W2 + b2
        mu = jnp.mean(h, axis=0)
        var = jnp.var(h, axis=0)
        h = (h - mu) * jax.lax.rsqrt(var + BN_EPS) * gamma + beta
        return jax.nn.relu(h) + x
    edge_index = jnp.stack([src, dst])
    x = _layernorm(x + _L0_gnn_ref(x, edge_attr_64, L0_gnn_We, L0_gnn_be, L0_gnn_W1, L0_gnn_b1, L0_gnn_W2, L0_gnn_b2, L0_gnn_gamma, L0_gnn_beta, L0_gnn_eps, edge_index), axis=-1)
    return x

_drawn_inputs = setup_inputs


def setup_inputs(seed=0):
    import zlib

    import numpy as np

    out = dict(_drawn_inputs(seed))
    spreads = {'L0_gnn_be': (0.0, 0.1),
     'L0_gnn_b1': (0.0, 2.0),
     'L0_gnn_b2': (0.0, 2.0),
     'L0_gnn_gamma': (1.0, 0.2),
     'L0_gnn_beta': (0.0, 0.1)}
    factors = {}
    for name, (base, spread) in spreads.items():
        noise = np.random.default_rng([zlib.crc32(name.encode()), seed]).standard_normal(out[name].shape)
        drawn = base * np.exp(spread * noise) if base else spread * noise
        out[name] = jnp.asarray(drawn.astype(out[name].dtype))
    for name, factor in factors.items():
        out[name] = (out[name] * factor).astype(out[name].dtype)
    return out
```

```python
import concourse.bass as bass
from concourse import mybir
from contextlib import ExitStack


def gine_layer_kernel(
    nc: bass.Bass,
    x: bass.AP,
    xt: bass.AP,
    src_loop: bass.AP,
    src_col: bass.AP,
    dst_tiles: bass.AP,
    dst_last: bass.AP,
    eat: bass.AP,
    we: bass.AP,
    be: bass.AP,
    w1: bass.AP,
    b1: bass.AP,
    w2: bass.AP,
    b2: bass.AP,
    gamma: bass.AP,
    beta: bass.AP,
    eps: bass.AP,
    out: bass.AP,
):
    fp32 = mybir.dt.float32
    i32 = mybir.dt.int32
    ALU = mybir.AluOpType
    ACT = mybir.ActivationFunctionType
    AX = mybir.AxisListType

    P = 128
    N, HID = x.shape
    EDIM, E = eat.shape
    K = EDIM + 1
    BN_EPS = LN_EPS = 1e-5

    GROUP = 4
    WIN = 64
    SLOTS = 6
    HALF = GROUP * SLOTS // 2
    ITERS = src_loop.shape[0] // 2
    FULL = E // P
    REST = E - FULL * P
    GE = GROUP * P
    LOOPED = ITERS * SLOTS
    LASTT = FULL - LOOPED * GROUP
    GROUPS = LOOPED + 1
    LASTG = LOOPED
    assert 0 <= LASTT < GROUP and REST > 0

    NBLK = -(-N // P)
    GBLK = -(-GROUPS // P)
    CH = 500
    CHUNKS = [(c, min(CH, N - c)) for c in range(0, N, CH)]
    BATCHES = [(0, 13), (13, 12), (25, 12), (37, 12)]
    assert BATCHES[-1][0] + BATCHES[-1][1] == NBLK

    BANK = 512
    WALL = -(-N // BANK)
    SPLIT = [(0, 7), (7, WALL)]

    ctx = ExitStack()
    with ctx:
        def sb(name, shape, dt=fp32):
            return ctx.enter_context(nc.sbuf_tensor(name, shape, dt))

        def sem(name):
            return ctx.enter_context(nc.semaphore(name))

        accT = sb("accT", [HID, N + WIN])
        xT = sb("xT", [HID, N])
        ea = [sb(f"ea{h}", [K, HALF * P]) for h in range(2)]
        xg = sb("xg", [P, SLOTS, GROUP, HID])
        pre = sb("pre", [P, 2, GROUP, HID])
        msg = sb("msg", [P, 2, GROUP, HID])
        hot = sb("hot", [P, 2, GROUP, WIN])
        idxb = [sb(f"idxb{h}", [P, HALF], i32) for h in range(2)]
        idx_last = sb("idx_last", [P, GROUP], i32)
        dsti = sb("dsti", [P, FULL + 1], i32)
        rel = sb("rel", [P, FULL + 1])
        least = sb("least", [P, GROUPS])
        leastT = sb("leastT", [P, GBLK])
        diag = sb("diag", [P, GBLK, P])
        base = sb("base", [P, GROUPS])
        basei = sb("basei", [P, GROUPS], i32)
        over = sb("over", [P, 2])
        overT = sb("overT", [1, 1])
        flag = sb("flag", [1, 1], i32)
        iota_i = sb("iota_i", [P, WIN], i32)
        iota = sb("iota", [P, WIN])
        ident = sb("ident", [P, P])
        ones = sb("ones", [P, P])
        wea = sb("wea", [K, HID])
        w1s = sb("w1s", [HID, HID])
        w2s = sb("w2s", [HID, HID])
        par = sb("par", [HID, 5])
        b1s, b2s, gms, bts, eps1 = (par[:, j:j + 1] for j in range(5))
        h1 = sb("h1", [HID, 2, BANK])
        bnst = sb("bnst", [HID, len(CHUNKS), 6])
        bn = sb("bn", [HID, 8])
        lnst = sb("lnst", [P, NBLK, 6])
        ln = sb("ln", [P, 6, NBLK])
        y = sb("y", [P, 2, 13, HID])
        hot_all = sb("hot_all", [P, N])
        iota_all = sb("iota_all", [P, N])
        g_idx = sb("g_idx", [P, 1], i32)
        g_ea = sb("g_ea", [K, P])
        g_xg = sb("g_xg", [P, HID])
        g_msg = sb("g_msg", [P, HID])
        g_dst = sb("g_dst", [P, 4])

        ps = ctx.enter_context(nc.psum_tensor("ps", [P, 8, BANK], fp32))

        def ps_lin(k):
            return ps[:, k, :].rearrange("p (t n) -> p t n", t=GROUP)

        def ps_win(k):
            return ps[:, 2 + k, 0:WIN]

        s_const = sem("s_const")
        s_apart = sem("s_apart")
        s_small = sem("s_small")
        s_dst = sem("s_dst")
        s_xt = sem("s_xt")
        s_ea = [sem("s_ea0"), sem("s_ea1")]
        s_idx = [sem("s_idx0"), sem("s_idx1")]
        s_xg = [sem(f"s_xg{g}") for g in range(SLOTS)]
        s_last = sem("s_last")
        s_pro = sem("s_pro")
        s_tr = sem("s_tr")
        s_init = sem("s_init")
        s_lin = sem("s_lin")
        s_pre = sem("s_pre")
        s_msg = sem("s_msg")
        s_hot = sem("s_hot")
        s_win = sem("s_win")
        s_acc = sem("s_acc")
        s_flag = sem("s_flag")
        g_const = sem("g_const")
        g_load = sem("g_load")
        g_gat = sem("g_gat")
        g_lin = sem("g_lin")
        g_vec = sem("g_vec")
        g_sum = sem("g_sum")
        s_agg = sem("s_agg")
        s_m1 = sem("s_m1")
        s_h1 = sem("s_h1")
        s_m2 = sem("s_m2")
        s_h2 = sem("s_h2")
        s_st = sem("s_st")
        s_bn = sem("s_bn")
        s_sd = sem("s_sd")
        s_relu = sem("s_relu")
        s_z = sem("s_z")
        s_zt = sem("s_zt")
        s_ln = sem("s_ln")
        s_lsd = sem("s_lsd")
        s_y = sem("s_y")
        s_out = [sem(f"s_out{n}") for n in range(len(BATCHES))]

        block = ctx.enter_context(nc.Block())

        def wait_apart(eng, semaphore, value):
            eng.wait_ge(semaphore, value)
            eng.sem_inc(s_apart, 1)

        LAST = [(j, P) for j in range(LASTT)] + [(LASTT, REST)]
        LAST_E0 = LASTG * GE

        @block.sync
        def _(sp):
            def load_half(i, h):
                sp.dma_start(idxb[h][:, :], src_loop[2 * i + h]).then_inc(s_idx[h], 16)
                sp.dma_start(ea[h][0:EDIM, :], eat[:, bass.ds((2 * i + h) * (HALF * P), HALF * P)])\
                  .then_inc(s_ea[h], 16)

            load_half(0, 0)
            sp.dma_start(dsti[:, 0:FULL], dst_tiles).then_inc(s_dst, 16)
            sp.dma_start(dsti[0:REST, FULL:FULL + 1], dst_last).then_inc(s_dst, 16)
            load_half(0, 1)
            for j, r in LAST:
                e0 = LAST_E0 + j * P
                sp.dma_start(idx_last[0:r, j:j + 1], src_col[e0:e0 + r, :]).then_inc(s_last, 16)
            with sp.Fori(1, ITERS) as i:
                for h in range(2):
                    for g in range(h * SLOTS // 2, (h + 1) * SLOTS // 2):
                        wait_apart(sp, s_xg[g], i * (16 * GROUP))
                    wait_apart(sp, s_lin, (i - 1) * SLOTS + (h + 1) * (SLOTS // 2))
                    load_half(i, h)
            sp.wait_ge(s_lin, (ITERS - 1) * SLOTS + SLOTS // 2)
            sp.dma_start(ea[0][0:EDIM, 0:E - LAST_E0], eat[:, LAST_E0:E]).then_inc(s_ea[0], 16)

            sp.wait_ge(s_flag, 1)
            many = sp.value_load(flag[0:1, 0:1], min_val=0, max_val=1)
            with sp.If(many > 0):
                def tile(t, r, n):
                    wait_apart(sp, g_sum, n * len(SPLIT))
                    sp.dma_start(g_idx[0:r, :], src_col[bass.ds(t * P, r), :]).then_inc(g_load, 16)
                    sp.dma_start(g_ea[0:EDIM, 0:r], eat[:, bass.ds(t * P, r)]).then_inc(g_load, 16)

                sp.dma_start(g_idx[0:P, :], src_col[0:P, :]).then_inc(g_load, 16)
                sp.dma_start(g_ea[0:EDIM, 0:P], eat[:, 0:P]).then_inc(g_load, 16)
                with sp.Fori(1, FULL) as t:
                    tile(t, P, t)
                tile(FULL, REST, FULL)

            for n, (b0, nb) in enumerate(BATCHES):
                sp.wait_ge(s_y, n + 1)
                whole = nb if (b0 + nb) * P <= N else nb - 1
                sp.dma_start(out[b0 * P:(b0 + whole) * P, :].rearrange("(b p) h -> p b h", p=P),
                             y[:, n % 2, 0:whole, :]).then_inc(s_out[n], 16)
                if whole < nb:
                    rows = N - (b0 + whole) * P
                    sp.dma_start(out[(b0 + whole) * P:N, :], y[0:rows, n % 2, whole, :]).then_inc(s_out[n], 16)
            for n in range(len(BATCHES)):
                sp.wait_ge(s_out[n], 16 if n + 1 < len(BATCHES) or N % P == 0 else 32)

        @block.gpsimd
        def _(pool):
            pool.memset(ident[:, :], 0.0).then_inc(s_const, 1)
            pool.iota(iota_i[:, :], pattern=[[1, WIN]], base=0, channel_multiplier=0).then_inc(s_const, 1)
            pool.wait_ge(s_const, 2)
            pool.affine_select(out=ident[:, :], in_=ident[:, :], compare_op=ALU.not_equal, fill=1.0,
                               base=0, pattern=[[-1, P]], channel_multiplier=1).then_inc(s_const, 1)

            def gather(slot, j, rows, index, done):
                pool.indirect_dma_start(
                    out=xg[0:rows, slot, j, :], out_offset=None, in_=x,
                    in_offset=bass.IndirectOffsetOnAxis(ap=index, axis=0)).then_inc(done, 16)

            def iteration(i, first):
                for g in range(SLOTS):
                    h, at = divmod(g * GROUP, HALF)
                    if at == 0:
                        wait_apart(pool, s_idx[h], (i + 1) * 16)
                    if not first:
                        wait_apart(pool, s_pre, (i - 1) * SLOTS + g + 1)
                    for j in range(GROUP):
                        gather(g, j, P, idxb[h][:, at + j:at + j + 1], s_xg[g])

            iteration(0, True)
            with pool.Fori(1, ITERS) as i:
                iteration(i, False)
            pool.wait_ge(s_last, 16 * len(LAST))
            pool.wait_ge(s_pre, (ITERS - 1) * SLOTS + 1)
            for j, r in LAST:
                gather(0, j, r, idx_last[0:r, j:j + 1], s_xg[0])

            pool.wait_ge(s_flag, 1)
            many = pool.value_load(flag[0:1, 0:1], min_val=0, max_val=1)
            with pool.If(many > 0):
                pool.iota(iota_all[:, :].bitcast(i32), pattern=[[1, N]], base=0, channel_multiplier=0)\
                    .then_inc(g_const, 1)

                def tile(r, n):
                    wait_apart(pool, g_load, (n + 1) * 32)
                    pool.indirect_dma_start(
                        out=g_xg[0:r, :], out_offset=None, in_=x,
                        in_offset=bass.IndirectOffsetOnAxis(ap=g_idx[0:r, :], axis=0)).then_inc(g_gat, 16)

                with pool.Fori(0, FULL) as t:
                    tile(P, t)
                tile(REST, FULL)
            pool.nop()

        @block.scalar
        def _(act):
            act.dma_start(wea[0:EDIM, :], we).then_inc(s_small, 16)
            act.dma_start(wea[EDIM:K, :], be).then_inc(s_small, 16)
            act.dma_start(eps1, eps.partition_broadcast(P)).then_inc(s_small, 16)
            act.dma_start(xT[:, :], xt).then_inc(s_xt, 16)
            for j, v in enumerate((b1, b2, gamma, beta)):
                act.dma_start(par[:, j:j + 1], v).then_inc(s_small, 16)
            act.dma_start(w1s[:, :], w1).then_inc(s_small, 16)
            act.dma_start(w2s[:, :], w2).then_inc(s_small, 16)
            act.wait_ge(s_xt, 16)
            act.wait_ge(s_pro, 1)
            act.activation(accT[:, 0:N], xT[:, :], ACT.Copy, scale=bn[:, 7:8]).then_inc(s_init, 1)

            def relu(n, k, shape=None):
                act.activation(msg[:, k, :, :], pre[:, k, :, :], ACT.Relu).then_inc(s_msg, 1)

            def iteration(i, first):
                for g in range(SLOTS):
                    n = i * SLOTS + g
                    act.wait_ge(s_pre, n + 1)
                    if not first or g >= 2:
                        act.wait_ge(s_win, n - 1)
                    relu(n, g % 2)

            iteration(0, True)
            with act.Fori(1, ITERS) as i:
                iteration(i, False)
            act.wait_ge(s_pre, LASTG + 1)
            act.wait_ge(s_win, LASTG - 1)
            k = LASTG % 2
            act.activation(msg[:, k, 0:LASTT, :], pre[:, k, 0:LASTT, :], ACT.Relu).then_inc(s_msg, 1)
            act.activation(msg[0:REST, k, LASTT, :], pre[0:REST, k, LASTT, :], ACT.Relu).then_inc(s_msg, 1)

            for c, (c0, w) in enumerate(CHUNKS):
                act.wait_ge(s_m1, c + 1)
                if c >= 2:
                    act.wait_ge(s_m2, c - 1)
                act.activation(h1[:, c % 2, 0:w], ps[:, c % 2, 0:w], ACT.Relu, bias=b1s).then_inc(s_h1, 1)
                if c >= 1:
                    p0, pw = CHUNKS[c - 1]
                    act.wait_ge(s_m2, c)
                    act.activation(accT[:, p0:p0 + pw], ps[:, 2 + (c - 1) % 2, 0:pw], ACT.Identity, bias=b2s)\
                       .then_inc(s_h2, 1)
            c = len(CHUNKS) - 1
            act.wait_ge(s_m2, c + 1)
            act.activation(accT[:, CHUNKS[c][0]:N], ps[:, 2 + c % 2, 0:CHUNKS[c][1]], ACT.Identity, bias=b2s)\
               .then_inc(s_h2, 1)
            act.wait_ge(s_bn, 1)
            act.activation(bn[:, 3:4], bn[:, 2:3], ACT.Sqrt).then_inc(s_sd, 1)
            act.wait_ge(s_bn, 2)
            for n, (b0, nb) in enumerate(BATCHES):
                a, b = b0 * P, min(N, (b0 + nb) * P)
                act.activation(accT[:, a:b], accT[:, a:b], ACT.Relu, scale=bn[:, 4:5], bias=bn[:, 6:7])\
                   .then_inc(s_relu, 1)
            for n, (b0, nb) in enumerate(BATCHES):
                act.wait_ge(s_ln, 2 * n + 1)
                act.activation(ln[:, 2, b0:b0 + nb], ln[:, 1, b0:b0 + nb], ACT.Sqrt).then_inc(s_lsd, 1)
                act.wait_ge(s_ln, 2 * n + 2)
                if n >= 2:
                    act.wait_ge(s_out[n - 2], 16)
                for b in range(b0, b0 + nb):
                    r = min(P, N - b * P)
                    last = act.activation(y[0:r, n % 2, b - b0, :],
                                          ps[0:r, 4 * (n % 2) + (b - b0) // 4, (b - b0) % 4 * P:((b - b0) % 4 + 1) * P],
                                          ACT.Identity, scale=ln[0:r, 3, b:b + 1], bias=ln[0:r, 4, b:b + 1])
                last.then_inc(s_y, 1)

        @block.vector
        def _(dve):
            done = [0]

            def step(ins):
                done[0] += 1
                ins.then_inc(s_pro, 1)
                dve.wait_ge(s_pro, done[0])

            for h in range(2):
                dve.memset(ea[h][EDIM:K, :], 1.0)
            dve.wait_ge(s_small, 16 * 9)
            step(dve.tensor_scalar_add(bn[:, 7:8], eps1, 1.0))
            dve.memset(accT[:, N:N + WIN], 0.0).then_inc(s_init, 1)
            dve.memset(ones[:, :], 1.0)
            dve.memset(lnst[:, NBLK - 1, :], 0.0)
            dve.memset(leastT[:, :], 0.0)
            dve.wait_ge(s_dst, 32)
            step(dve.memset(least[:, LASTG:GROUPS], float(N)))
            dve.tensor_copy(rel[0:REST, FULL:FULL + 1], dsti[0:REST, FULL:FULL + 1])
            step(dve.tensor_copy(rel[:, 0:FULL], dsti[:, 0:FULL]))
            dve.tensor_reduce(least[:, 0:LOOPED], rel[:, 0:LOOPED * GROUP].rearrange("p (g t) -> p g t", t=GROUP),
                              AX.X, ALU.min)
            if LASTT:
                step(dve.tensor_reduce(least[:, LASTG:GROUPS], rel[:, LOOPED * GROUP:FULL], AX.X, ALU.min))
            step(dve.tensor_tensor(least[0:REST, LASTG:GROUPS], least[0:REST, LASTG:GROUPS],
                                   rel[0:REST, FULL:FULL + 1], ALU.min))
            dve.nop().then_inc(s_tr, 1)
            dve.wait_ge(s_tr, 2)
            for b in range(GBLK):
                w = min(P, GROUPS - b * P)
                last = dve.tensor_reduce(leastT[0:w, b:b + 1], ps[0:w, b, 0:P], AX.X, ALU.min)
            step(last)
            dve.wait_ge(s_const, 3)
            for b in range(GBLK):
                last = dve.tensor_scalar(diag[:, b, :], ident[:, :], leastT[:, b:b + 1], None, ALU.mult)
            last.then_inc(s_tr, 1)
            dve.wait_ge(s_tr, 4)
            step(dve.tensor_copy(base[:, :], ps[:, 4, 0:GROUPS]))
            dve.tensor_copy(basei[:, :], base[:, :])
            dve.tensor_copy(iota[:, :], iota_i[:, :])
            v = rel[:, 0:LOOPED * GROUP].rearrange("p (g t) -> p g t", t=GROUP)
            dve.tensor_tensor(v, v, base[:, 0:LOOPED].unsqueeze(2).to_broadcast([P, LOOPED, GROUP]), ALU.subtract)
            if LASTT:
                dve.tensor_scalar(rel[:, LOOPED * GROUP:FULL], rel[:, LOOPED * GROUP:FULL],
                                  base[:, LASTG:GROUPS], None, ALU.subtract)
            step(dve.tensor_scalar(rel[0:REST, FULL:FULL + 1], rel[0:REST, FULL:FULL + 1],
                                   base[0:REST, LASTG:GROUPS], None, ALU.subtract))
            step(dve.tensor_reduce(over[:, 0:1], rel[:, 0:FULL], AX.X, ALU.max))
            step(dve.tensor_tensor(over[0:REST, 0:1], over[0:REST, 0:1], rel[0:REST, FULL:FULL + 1], ALU.max))
            dve.nop().then_inc(s_tr, 1)
            dve.wait_ge(s_tr, 6)
            step(dve.tensor_reduce(overT[0:1, 0:1], ps[0:1, 5, 0:P], AX.X, ALU.max))
            dve.tensor_scalar(flag[0:1, 0:1], overT[0:1, 0:1], float(WIN), None, ALU.is_ge).then_inc(s_flag, 1)
            dve.nop().then_inc(s_tr, 1)

            def one_hot(n, k, first):
                if not first:
                    dve.wait_ge(s_win, n - 1)
                t0 = n * GROUP
                dve.tensor_tensor(
                    hot[:, k, :, :],
                    rel[:, bass.ds(t0, GROUP)].unsqueeze(2).to_broadcast([P, GROUP, WIN]),
                    iota[:, :].unsqueeze(1).to_broadcast([P, GROUP, WIN]), ALU.is_equal).then_inc(s_hot, 1)

            def add_x(i, g, n, first):
                dve.wait_ge(s_lin, n + 1)
                dve.wait_ge(s_xg[g], (i + 1) * (16 * GROUP))
                if not first:
                    dve.wait_ge(s_msg, n - 1)
                dve.tensor_tensor(pre[:, g % 2, :, :], ps_lin(g % 2), xg[:, g, :, :], ALU.add).then_inc(s_pre, 1)

            def add_window(n, k, first=False):
                at = dve.value_load(basei[0:1, bass.ds(n, 1)], min_val=0, max_val=N - 1)
                dve.wait_ge(s_win, n + 1)
                if not first:
                    dve.wait_ge(s_acc, n)
                dve.tensor_tensor(accT[:, bass.ds(at, WIN)], accT[:, bass.ds(at, WIN)], ps_win(k), ALU.add)\
                   .then_inc(s_acc, 1)

            def iteration(i, first):
                for g in range(SLOTS):
                    n = i * SLOTS + g
                    one_hot(n, g % 2, first and g < 2)
                    add_x(i, g, n, first and g < 2)
                    if not first or g >= 1:
                        if first and g == 1:
                            dve.wait_ge(s_init, 2)
                        add_window(n - 1, (g - 1) % 2, first and g == 1)

            iteration(0, True)
            with dve.Fori(1, ITERS) as i:
                iteration(i, False)
            n, k = LASTG, LASTG % 2
            dve.wait_ge(s_win, n - 1)
            for j, r in LAST:
                last = dve.tensor_scalar(hot[0:r, k, j, :], iota[0:r, :], rel[0:r, LOOPED * GROUP + j:LOOPED * GROUP + j + 1],
                                         None, ALU.is_equal)
            last.then_inc(s_hot, 1)
            dve.wait_ge(s_lin, n + 1)
            dve.wait_ge(s_xg[0], ITERS * (16 * GROUP) + 16 * len(LAST))
            dve.wait_ge(s_msg, n - 1)
            for j, r in LAST:
                last = dve.tensor_tensor(pre[0:r, k, j, :], ps_lin(k)[0:r, j, :], xg[0:r, 0, j, :], ALU.add)
            last.then_inc(s_pre, 1)
            add_window(n - 1, (n - 1) % 2)
            add_window(n, k)
            dve.wait_ge(s_acc, GROUPS)

            many = dve.value_load(flag[0:1, 0:1], min_val=0, max_val=1)
            with dve.If(many > 0):
                dve.memset(g_ea[EDIM:K, :], 1.0).then_inc(g_const, 1)
                dve.wait_ge(g_const, 2)
                dve.tensor_copy(iota_all[:, :], iota_all[:, :].bitcast(i32)).then_inc(g_const, 1)
                dve.wait_ge(g_const, 3)
                STEPS = 8

                def tile(t, g, r, n):
                    def wait(k):
                        dve.wait_ge(g_vec, n * STEPS + k)
                    dve.tensor_scalar(g_dst[0:r, 0:1], rel[0:r, bass.ds(t, 1)], float(WIN), None, ALU.is_ge)\
                       .then_inc(g_vec, 1)
                    dve.tensor_scalar(g_dst[0:r, 1:2], rel[0:r, bass.ds(t, 1)], base[0:r, bass.ds(g, 1)], 1.0,
                                      ALU.add, ALU.add).then_inc(g_vec, 1)
                    wait(2)
                    dve.tensor_tensor(g_dst[0:r, 2:3], g_dst[0:r, 0:1], g_dst[0:r, 1:2], ALU.mult).then_inc(g_vec, 1)
                    wait(3)
                    dve.tensor_scalar_add(g_dst[0:r, 3:4], g_dst[0:r, 2:3], -1.0).then_inc(g_vec, 1)
                    wait(4)
                    dve.tensor_scalar(hot_all[0:r, :], iota_all[0:r, :], g_dst[0:r, 3:4], None, ALU.is_equal)
                    dve.wait_ge(g_lin, n + 1)
                    dve.wait_ge(g_gat, (n + 1) * 16)
                    dve.tensor_tensor(g_msg[0:r, :], ps[0:r, 7, 0:HID], g_xg[0:r, :], ALU.add).then_inc(g_vec, 1)
                    wait(5)
                    dve.tensor_scalar_max(g_msg[0:r, :], g_msg[0:r, :], 0.0).then_inc(g_vec, 1)
                    for m, (a, b) in enumerate(SPLIT):
                        dve.wait_ge(g_sum, n * len(SPLIT) + m + 1)
                        c0, c1 = a * BANK, min(N, b * BANK)
                        dve.tensor_tensor(accT[:, c0:c1], accT[:, c0:c1],
                                          ps[:, 0:b - a, :].rearrange("p a n -> p (a n)")[:, 0:c1 - c0], ALU.add)\
                           .then_inc(g_vec, 1)
                    wait(STEPS)

                with dve.Fori(0, LOOPED) as g:
                    for j in range(GROUP):
                        tile(g * GROUP + j, g, P, g * GROUP + j)
                for j, r in LAST:
                    tile(LOOPED * GROUP + j, LASTG, r, LOOPED * GROUP + j)
            dve.nop().then_inc(s_agg, 1)

            for c, (c0, w) in enumerate(CHUNKS):
                dve.wait_ge(s_h2, c + 1)
                dve.bn_stats(bnst[:, c, :], accT[:, c0:c0 + w]).then_inc(s_st, 1)
            dve.wait_ge(s_st, len(CHUNKS))
            done[0] = len(CHUNKS)

            def stat(ins):
                done[0] += 1
                ins.then_inc(s_st, 1)
                dve.wait_ge(s_st, done[0])

            stat(dve.bn_aggr(bn[:, 0:2], bnst[:, :, :].rearrange("p a b -> p (a b)")))
            dve.tensor_scalar_add(bn[:, 2:3], bn[:, 1:2], BN_EPS).then_inc(s_bn, 1)
            dve.wait_ge(s_sd, 1)
            stat(dve.reciprocal(bn[:, 5:6], bn[:, 3:4]))
            stat(dve.tensor_tensor(bn[:, 4:5], bn[:, 5:6], gms, ALU.mult))
            stat(dve.tensor_tensor(bn[:, 2:3], bn[:, 4:5], bn[:, 0:1], ALU.mult))
            dve.tensor_tensor(bn[:, 6:7], bts, bn[:, 2:3], ALU.subtract).then_inc(s_bn, 1)

            def residual(n):
                b0, nb = BATCHES[n]
                a, b = b0 * P, min(N, (b0 + nb) * P)
                dve.wait_ge(s_relu, n + 1)
                dve.scalar_tensor_tensor(out=accT[:, a:b], in0=xT[:, a:b], scalar=2.0, in1=accT[:, a:b],
                                         op0=ALU.mult, op1=ALU.add).then_inc(s_z, 1)

            residual(0)
            for n, (b0, nb) in enumerate(BATCHES):
                if n + 1 < len(BATCHES):
                    residual(n + 1)
                dve.wait_ge(s_zt, n + 1)
                for b in range(b0, b0 + nb):
                    r = min(P, N - b * P)
                    last = dve.bn_stats(lnst[0:r, b, :],
                                        ps[0:r, 4 * (n % 2) + (b - b0) // 4, (b - b0) % 4 * P:((b - b0) % 4 + 1) * P])
                stat(last)
                me, qe, mo, qo = (lnst[:, b0:b0 + nb, j] for j in (1, 2, 4, 5))
                m, v, t, u, w = (ln[:, j, b0:b0 + nb] for j in (0, 1, 5, 3, 4))
                dve.tensor_tensor(m, me, mo, ALU.add)
                dve.tensor_tensor(t, me, mo, ALU.subtract)
                stat(dve.tensor_tensor(v, qe, qo, ALU.add))
                stat(dve.scalar_tensor_tensor(out=t, in0=t, scalar=0.25, in1=t, op0=ALU.mult, op1=ALU.mult))
                stat(dve.scalar_tensor_tensor(out=v, in0=v, scalar=1.0 / HID, in1=t, op0=ALU.mult, op1=ALU.add))
                stat(dve.tensor_scalar_add(v, v, LN_EPS))
                dve.nop().then_inc(s_ln, 1)
                dve.wait_ge(s_lsd, n + 1)
                stat(dve.reciprocal(u, ln[:, 2, b0:b0 + nb]))
                dve.scalar_tensor_tensor(out=w, in0=m, scalar=-0.5, in1=u, op0=ALU.mult, op1=ALU.mult)\
                   .then_inc(s_ln, 1)

        @block.tensor
        def _(pe):
            pe.wait_ge(s_const, 3)
            pe.wait_ge(s_tr, 1)
            for b in range(GBLK):
                w = min(P, GROUPS - b * P)
                last = pe.transpose(ps[0:w, b, 0:P], least[:, b * P:b * P + w], ident[:, :])
            last.then_inc(s_tr, 1)
            pe.wait_ge(s_tr, 3)
            for b in range(GBLK):
                w = min(P, GROUPS - b * P)
                last = pe.matmul(ps[:, 4, b * P:b * P + w], ones[:, :], diag[:, b, 0:w], start=True, stop=True)
            last.then_inc(s_tr, 1)
            pe.wait_ge(s_tr, 5)
            pe.transpose(ps[0:1, 5, 0:P], over[:, 0:1], ident[:, :]).then_inc(s_tr, 1)
            pe.wait_ge(s_small, 16 * 9)
            pe.wait_ge(s_tr, 7)

            def linear(h, at, k, tiles):
                for j, r in tiles:
                    last = pe.matmul(ps_lin(k)[0:r, j, :], ea[h][:, (at + j) * P:(at + j) * P + r], wea[:, :],
                                     start=True, stop=True)
                last.then_inc(s_lin, 1)

            def window(k, tiles):
                for j, r in tiles:
                    last = pe.matmul(ps_win(k), msg[0:r, k, j, :], hot[0:r, k, j, :],
                                     start=(j == 0), stop=(j == len(tiles) - 1))
                last.then_inc(s_win, 1)

            ALL = [(j, P) for j in range(GROUP)]

            def window_of(n, k, first):
                pe.wait_ge(s_msg, n + 1)
                pe.wait_ge(s_hot, n + 1)
                if not first:
                    pe.wait_ge(s_acc, n - 1)
                window(k, ALL)

            def iteration(i, first):
                for g in range(SLOTS):
                    n = i * SLOTS + g
                    h, at = divmod(g * GROUP, HALF)
                    if at == 0:
                        pe.wait_ge(s_ea[h], (i + 1) * 16)
                    if not first or g >= 2:
                        pe.wait_ge(s_pre, n - 1)
                    linear(h, at, g % 2, ALL)
                    if not first or g >= 1:
                        window_of(n - 1, (g - 1) % 2, first and g < 3)

            iteration(0, True)
            with pe.Fori(1, ITERS) as i:
                iteration(i, False)
            pe.wait_ge(s_ea[0], (ITERS + 1) * 16)
            pe.wait_ge(s_pre, LASTG - 1)
            linear(0, 0, LASTG % 2, LAST)
            window_of(LASTG - 1, (LASTG - 1) % 2, False)
            pe.wait_ge(s_msg, LASTG + 2)
            pe.wait_ge(s_hot, LASTG + 1)
            pe.wait_ge(s_acc, LASTG - 1)
            window(LASTG % 2, LAST)

            pe.wait_ge(s_flag, 1)
            many = pe.value_load(flag[0:1, 0:1], min_val=0, max_val=1)
            with pe.If(many > 0):
                pe.wait_ge(g_const, 3)
                STEPS = 8

                def tile(r, n, first):
                    pe.wait_ge(g_load, (n + 1) * 32)
                    if not first:
                        pe.wait_ge(g_vec, n * STEPS)
                    pe.matmul(ps[0:r, 7, 0:HID], g_ea[:, 0:r], wea[:, :], start=True, stop=True).then_inc(g_lin, 1)
                    pe.wait_ge(g_vec, n * STEPS + 6)
                    for m, (a, b) in enumerate(SPLIT):
                        if m:
                            pe.wait_ge(g_vec, n * STEPS + 6 + m)
                        for q in range(a, b):
                            w = min(BANK, N - q * BANK)
                            last = pe.matmul(ps[:, q - a, 0:w], g_msg[0:r, :], hot_all[0:r, q * BANK:q * BANK + w],
                                             start=True, stop=True)
                        last.then_inc(g_sum, 1)

                tile(P, 0, True)
                with pe.Fori(1, FULL) as t:
                    tile(P, t, False)
                tile(REST, FULL, False)

            pe.wait_ge(s_agg, 1)
            for c, (c0, w) in enumerate(CHUNKS):
                if c >= 2:
                    pe.wait_ge(s_h1, c - 1)
                pe.matmul(ps[:, c % 2, 0:w], w1s[:, :], accT[:, c0:c0 + w], start=True, stop=True).then_inc(s_m1, 1)
                if c >= 1:
                    p0, pw = CHUNKS[c - 1]
                    pe.wait_ge(s_h1, c)
                    if c >= 3:
                        pe.wait_ge(s_h2, c - 2)
                    pe.matmul(ps[:, 2 + (c - 1) % 2, 0:pw], w2s[:, :], h1[:, (c - 1) % 2, 0:pw],
                              start=True, stop=True).then_inc(s_m2, 1)
            c = len(CHUNKS) - 1
            pe.wait_ge(s_h1, c + 1)
            pe.wait_ge(s_h2, c - 1)
            pe.matmul(ps[:, 2 + c % 2, 0:CHUNKS[c][1]], w2s[:, :], h1[:, c % 2, 0:CHUNKS[c][1]],
                      start=True, stop=True).then_inc(s_m2, 1)
            pe.wait_ge(s_h2, len(CHUNKS))
            for n, (b0, nb) in enumerate(BATCHES):
                pe.wait_ge(s_z, n + 1)
                if n >= 2:
                    pe.wait_ge(s_y, n - 1)
                for b in range(b0, b0 + nb):
                    r = min(P, N - b * P)
                    last = pe.transpose(
                        ps[0:r, 4 * (n % 2) + (b - b0) // 4, (b - b0) % 4 * P:((b - b0) % 4 + 1) * P],
                        accT[:, b * P:b * P + r], ident[:, :])
                last.then_inc(s_zt, 1)


def kernel(**inputs):
    import numpy as _np
    import concourse.bacc as _bacc
    from concourse import mybir as _mybir
    from concourse.bass_utils import run_bass_kernel_spmd as _run

    P, HALF = 128, 12
    a = {k: _np.asarray(v) for k, v in inputs.items()}
    x, src, dst, ea = a["x"], a["src"], a["dst"], a["edge_attr_64"]
    E = src.shape[0]
    full = E // P
    halves = full // (2 * HALF) * 2
    col = lambda v: v.reshape(-1, 1)
    data = {
        "x": x,
        "xt": x.T,
        "src_loop": src[:halves * HALF * P].reshape(halves, HALF, P).transpose(0, 2, 1),
        "src_col": col(src),
        "dst_tiles": dst[:full * P].reshape(full, P).T,
        "dst_last": col(dst[full * P:]),
        "eat": ea.T,
        "we": a["L0_gnn_We"],
        "be": a["L0_gnn_be"].reshape(1, -1),
        "w1": a["L0_gnn_W1"],
        "b1": col(a["L0_gnn_b1"]),
        "w2": a["L0_gnn_W2"],
        "b2": col(a["L0_gnn_b2"]),
        "gamma": col(a["L0_gnn_gamma"]),
        "beta": col(a["L0_gnn_beta"]),
        "eps": a["L0_gnn_eps"].reshape(1, 1),
    }
    nc = _bacc.Bacc("TRN2", target_bir_lowering=False, num_devices=1)
    arrays, args = {}, []
    for name, v in data.items():
        v = _np.ascontiguousarray(v)
        arrays[f"in_{name}"] = v
        args.append(nc.dram_tensor(f"in_{name}", v.shape, _mybir.dt.from_np(v.dtype), kind="ExternalInput").ap())
    args.append(nc.dram_tensor("out", x.shape, _mybir.dt.float32, kind="ExternalOutput").ap())
    gine_layer_kernel(nc, *args)
    r = _run(nc, [arrays], core_ids=[0])
    return r.results[0]["out"]
```

```python
import concourse.bass as bass
from concourse import mybir
from contextlib import ExitStack


def gine_layer_kernel(
    nc: bass.Bass,
    x: bass.AP,
    xt: bass.AP,
    src_loop: bass.AP,
    src_row: bass.AP,
    src_col: bass.AP,
    dst_tiles: bass.AP,
    dst_last: bass.AP,
    eat: bass.AP,
    we: bass.AP,
    be: bass.AP,
    w1: bass.AP,
    b1: bass.AP,
    w2: bass.AP,
    b2: bass.AP,
    gamma: bass.AP,
    beta: bass.AP,
    eps: bass.AP,
    out: bass.AP,
):
    fp32 = mybir.dt.float32
    i32 = mybir.dt.int32
    bf16 = mybir.dt.bfloat16
    ALU = mybir.AluOpType
    ACT = mybir.ActivationFunctionType
    AX = mybir.AxisListType

    P = 128
    N, HID = x.shape
    EDIM, E = eat.shape
    K = EDIM + 1
    BN_EPS = LN_EPS = 1e-5

    GROUP = 4
    WIN = 64
    SLOTS = 6
    HALF = GROUP * SLOTS // 2
    ITERS = src_loop.shape[0] // 2
    FULL = E // P
    REST = E - FULL * P
    GE = GROUP * P
    LOOPED = ITERS * SLOTS
    LASTT = FULL - LOOPED * GROUP
    GROUPS = LOOPED + 1
    LASTG = LOOPED
    assert 0 <= LASTT < GROUP and REST > 0

    NBLK = -(-N // P)
    GBLK = -(-GROUPS // P)
    CH = 500
    CHUNKS = [(c, min(CH, N - c)) for c in range(0, N, CH)]
    START = 2
    PIECE = -(-NBLK // (SLOTS - 1))
    PIECES = [(b, min(PIECE, NBLK - b)) for b in range(0, NBLK, PIECE)]
    NQ = len(PIECES)
    AHEAD = 2
    EARLY = AHEAD * SLOTS - 1
    EARLY_N = EARLY * CH
    BATCHES = [(0, 4), (4, 8), (12, 12), (24, 12), (36, 13)]
    assert BATCHES[-1][0] + BATCHES[-1][1] == NBLK and EARLY < len(CHUNKS) - 1

    BANK = 512
    WALL = -(-N // BANK)
    SPLIT = [(0, 7), (7, WALL)]

    ctx = ExitStack()
    with ctx:
        def sb(name, shape, dt=fp32):
            return ctx.enter_context(nc.sbuf_tensor(name, shape, dt))

        def sem(name):
            return ctx.enter_context(nc.semaphore(name))

        accT = sb("accT", [HID, N + WIN])
        xT = sb("xT", [HID, N])
        ea = [sb(f"ea{h}", [K, HALF * P]) for h in range(2)]
        xg = sb("xg", [P, SLOTS, GROUP, HID])
        pre = sb("pre", [P, 2, GROUP, HID])
        msg = sb("msg", [P, 2, GROUP, HID])
        hot = sb("hot", [P, 2, GROUP, WIN])
        idxb = [sb(f"idxb{h}", [P, HALF], i32) for h in range(2)]
        idx_last = sb("idx_last", [P, GROUP], i32)
        dsti = sb("dsti", [P, FULL + 1], i32)
        rel = sb("rel", [P, FULL + 1])
        least = sb("least", [P, GROUPS])
        leastT = sb("leastT", [P, GBLK])
        diag = sb("diag", [P, GBLK, P])
        base = sb("base", [P, GROUPS])
        basei = sb("basei", [P, GROUPS], i32)
        over = sb("over", [P, 2])
        overT = sb("overT", [1, 1])
        flag = sb("flag", [1, 2], i32)
        flagf = sb("flagf", [1, 4])
        iota_i = sb("iota_i", [P, WIN], i32)
        iota = sb("iota", [P, WIN])
        ident = sb("ident", [P, P])
        ones = sb("ones", [P, P])
        wea = sb("wea", [K, HID])
        w1s = sb("w1s", [HID, HID])
        w2s = sb("w2s", [HID, HID])
        par = sb("par", [HID, 5])
        b1s, b2s, gms, bts, eps1 = (par[:, j:j + 1] for j in range(5))
        x3 = sb("x3", [P, NBLK, 3, HID], bf16)
        node = sb("node", [P, NBLK], i32)
        srcb = sb("srcb", [P, P], i32)
        sel = sb("sel", [P, 2, PIECE, P], bf16)
        got = sb("got", [P, 3, HID])
        h1 = sb("h1", [HID, 2, BANK])
        bnst = sb("bnst", [HID, len(CHUNKS), 6])
        bn = sb("bn", [HID, 8])
        lnst = sb("lnst", [P, NBLK, 6])
        ln = sb("ln", [P, 6, NBLK])
        hot_all = sb("hot_all", [P, N])
        iota_all = sb("iota_all", [P, NBLK * HID])
        h2 = hot_all
        y = iota_all[:, :].rearrange("p (b h) -> p b h", h=HID)
        xrow = y
        g_idx = sb("g_idx", [P, 1], i32)
        g_ea = sb("g_ea", [K, P])
        g_xg = sb("g_xg", [P, HID])
        g_msg = sb("g_msg", [P, HID])
        g_dst = sb("g_dst", [P, 4])

        ps = ctx.enter_context(nc.psum_tensor("ps", [P, 8, BANK], fp32))

        def ps_lin(k):
            return ps[:, k, :].rearrange("p (t n) -> p t n", t=GROUP)

        def ps_win(k):
            return ps[:, 2 + k, 0:WIN]

        s_xrow = sem("s_xrow")
        s_part = sem("s_part")
        s_rest = sem("s_rest")
        s_srcb = sem("s_srcb")
        s_sel = sem("s_sel")
        s_got = sem("s_got")
        s_lo = sem("s_lo")
        s_dve = sem("s_dve")
        s_const = sem("s_const")
        s_apart = sem("s_apart")
        s_small = sem("s_small")
        s_dst = sem("s_dst")
        s_xt = sem("s_xt")
        s_ea = [sem("s_ea0"), sem("s_ea1")]
        s_idx = [sem("s_idx0"), sem("s_idx1")]
        s_xg = [sem(f"s_xg{g}") for g in range(SLOTS)]
        s_last = sem("s_last")
        s_pro = sem("s_pro")
        s_tr = sem("s_tr")
        s_we = sem("s_we")
        s_init = sem("s_init")
        s_lin = sem("s_lin")
        s_pre = sem("s_pre")
        s_msg = sem("s_msg")
        s_hot = sem("s_hot")
        s_win = sem("s_win")
        s_acc = sem("s_acc")
        s_flag = sem("s_flag")
        g_const = sem("g_const")
        g_load = sem("g_load")
        g_gat = sem("g_gat")
        g_lin = sem("g_lin")
        g_vec = sem("g_vec")
        g_sum = sem("g_sum")
        s_agg = sem("s_agg")
        s_m1 = [sem("s_m1"), sem("r_m1")]
        s_h1 = [sem("s_h1"), sem("r_h1")]
        s_m2 = [sem("s_m2"), sem("r_m2")]
        s_h2 = [sem("s_h2"), sem("r_h2")]
        s_redone = sem("s_redone")
        s_st = sem("s_st")
        s_bn = sem("s_bn")
        s_sd = sem("s_sd")
        s_relu = sem("s_relu")
        s_z = sem("s_z")
        s_zt = sem("s_zt")
        s_ln = sem("s_ln")
        s_lsd = sem("s_lsd")
        s_y = sem("s_y")
        s_out = sem("s_out")

        block = ctx.enter_context(nc.Block())

        def wait_apart(eng, semaphore, value):
            eng.wait_ge(semaphore, value)
            eng.sem_inc(s_apart, 1)

        LAST = [(j, P) for j in range(LASTT)] + [(LASTT, REST)]
        LAST_E0 = LASTG * GE

        def special(i):
            return not isinstance(i, int) or START <= i < ITERS - AHEAD

        def gathered(i, g):
            if g < SLOTS - 1:
                return (i + 1) * (16 * GROUP)
            if not special(i):
                skipped = ITERS - AHEAD - START if i >= START else 0
                return (i + 1) * (16 * GROUP) - 16 * skipped
            return i * (16 * (GROUP - 1)) + (16 * GROUP + 16 * (START - 1))

        def before(i, g):
            if isinstance(i, int) or g < SLOTS - 1:
                return gathered(i - 1, g)
            return i * (16 * (GROUP - 1)) + 16 * START

        def run(eng, iteration):
            for i in range(START + 1):
                iteration(i)
            with eng.Fori(START + 1, ITERS - AHEAD) as i:
                iteration(i)
            for i in range(ITERS - AHEAD, ITERS):
                iteration(i)

        def edge(i, g):
            if not isinstance(i, int) or i < ITERS - AHEAD:
                return None
            return (i - (ITERS - AHEAD)) * SLOTS + g

        def zt(b, rows):
            return ps[0:rows, b // 4 % 8, b % 4 * P:(b % 4 + 1) * P]

        @block.sync
        def _(sp):
            def load_half(i, h):
                sp.dma_start(idxb[h][:, :], src_loop[2 * i + h]).then_inc(s_idx[h], 16)
                sp.dma_start(ea[h][0:EDIM, :], eat[:, bass.ds((2 * i + h) * (HALF * P), HALF * P)])\
                  .then_inc(s_ea[h], 16)

            sp.dma_start(idxb[0][:, :], src_loop[0]).then_inc(s_idx[0], 16)
            sp.dma_start(dsti[:, 0:FULL], dst_tiles).then_inc(s_dst, 16)
            sp.dma_start(dsti[0:REST, FULL:FULL + 1], dst_last).then_inc(s_dst, 16)
            sp.dma_start(ea[0][0:EDIM, :], eat[:, 0:HALF * P]).then_inc(s_ea[0], 16)
            load_half(0, 1)
            for j, r in LAST:
                e0 = LAST_E0 + j * P
                sp.dma_start(idx_last[0:r, j:j + 1], src_col[e0:e0 + r, :]).then_inc(s_last, 16)
            def load_srcb(i):
                tile = i * (GROUP * SLOTS) + (GROUP * SLOTS - 1)
                sp.dma_start(srcb[:, :], src_row[:, bass.ds(tile * P, P)].partition_broadcast(P))\
                  .then_inc(s_srcb, 16)

            def iteration(i):
                if isinstance(i, int) and i == 0:
                    return
                for h in range(2):
                    for g in range(h * SLOTS // 2, (h + 1) * SLOTS // 2):
                        wait_apart(sp, s_xg[g], before(i, g))
                    wait_apart(sp, s_lin, (i - 1) * SLOTS + (h + 1) * (SLOTS // 2))
                    load_half(i, h)
                    if h == 0 and special(i):
                        if not isinstance(i, int) or i > START:
                            wait_apart(sp, s_sel, (i - START) * NQ)
                        load_srcb(i)

            run(sp, iteration)
            sp.wait_ge(s_lin, (ITERS - 1) * SLOTS + SLOTS // 2)
            sp.dma_start(ea[0][0:EDIM, 0:E - LAST_E0], eat[:, LAST_E0:E]).then_inc(s_ea[0], 16)

            sp.wait_ge(s_flag, 1)
            many = sp.value_load(flag[0:1, 0:1], min_val=0, max_val=1)
            with sp.If(many > 0):
                def tile(t, r, n):
                    wait_apart(sp, g_sum, n * len(SPLIT))
                    sp.dma_start(g_idx[0:r, :], src_col[bass.ds(t * P, r), :]).then_inc(g_load, 16)
                    sp.dma_start(g_ea[0:EDIM, 0:r], eat[:, bass.ds(t * P, r)]).then_inc(g_load, 16)

                sp.dma_start(g_idx[0:P, :], src_col[0:P, :]).then_inc(g_load, 16)
                sp.dma_start(g_ea[0:EDIM, 0:P], eat[:, 0:P]).then_inc(g_load, 16)
                with sp.Fori(1, FULL) as t:
                    tile(t, P, t)
                tile(FULL, REST, FULL)

            for n, (b0, nb) in enumerate(BATCHES):
                sp.wait_ge(s_y, n + 1)
                whole = nb if (b0 + nb) * P <= N else nb - 1
                sp.dma_start(out[b0 * P:(b0 + whole) * P, :].rearrange("(b p) h -> p b h", p=P),
                             y[:, b0:b0 + whole, :]).then_inc(s_out, 16)
                if whole < nb:
                    rows = N - (b0 + whole) * P
                    sp.dma_start(out[(b0 + whole) * P:N, :], y[0:rows, b0 + whole, :]).then_inc(s_out, 16)
            sp.wait_ge(s_out, 16 * (len(BATCHES) + (N % P > 0)))

        @block.gpsimd
        def _(pool):
            pool.memset(ident[:, :], 0.0).then_inc(s_const, 1)
            pool.iota(iota_i[:, :], pattern=[[1, WIN]], base=0, channel_multiplier=0).then_inc(s_const, 1)
            pool.iota(node[:, :], pattern=[[P, NBLK]], base=0, channel_multiplier=1).then_inc(s_const, 1)
            pool.wait_ge(s_const, 3)
            pool.affine_select(out=ident[:, :], in_=ident[:, :], compare_op=ALU.not_equal, fill=1.0,
                               base=0, pattern=[[-1, P]], channel_multiplier=1).then_inc(s_const, 1)

            def gather(slot, j, rows, index, done):
                pool.indirect_dma_start(
                    out=xg[0:rows, slot, j, :], out_offset=None, in_=x,
                    in_offset=bass.IndirectOffsetOnAxis(ap=index, axis=0)).then_inc(done, 16)

            def iteration(i):
                for g in range(SLOTS):
                    h, at = divmod(g * GROUP, HALF)
                    if at == 0:
                        wait_apart(pool, s_idx[h], (i + 1) * 16)
                    if not isinstance(i, int) or i:
                        wait_apart(pool, s_pre, (i - 1) * SLOTS + g + 1)
                    for j in range(GROUP - (special(i) and g == SLOTS - 1)):
                        gather(g, j, P, idxb[h][:, at + j:at + j + 1], s_xg[g])

            run(pool, iteration)
            pool.wait_ge(s_last, 16 * len(LAST))
            pool.wait_ge(s_pre, (ITERS - 1) * SLOTS + 1)
            for j, r in LAST:
                gather(0, j, r, idx_last[0:r, j:j + 1], s_xg[0])

            pool.wait_ge(s_flag, 1)
            many = pool.value_load(flag[0:1, 0:1], min_val=0, max_val=1)
            with pool.If(many > 0):
                pool.iota(iota_all[:, 0:N].bitcast(i32), pattern=[[1, N]], base=0, channel_multiplier=0)\
                    .then_inc(g_const, 1)

                def tile(r, n):
                    wait_apart(pool, g_load, (n + 1) * 32)
                    pool.indirect_dma_start(
                        out=g_xg[0:r, :], out_offset=None, in_=x,
                        in_offset=bass.IndirectOffsetOnAxis(ap=g_idx[0:r, :], axis=0)).then_inc(g_gat, 16)

                with pool.Fori(0, FULL) as t:
                    tile(P, t)
                tile(REST, FULL)
            pool.nop()

        @block.scalar
        def _(act):
            act.dma_start(wea[0:EDIM, :], we).then_inc(s_we, 16)
            act.dma_start(wea[EDIM:K, :], be).then_inc(s_we, 16)
            act.dma_start(eps1, eps.partition_broadcast(P)).then_inc(s_we, 16)
            act.dma_start(xT[:, :], xt).then_inc(s_xt, 16)
            for j, v in enumerate((b1, b2, gamma, beta)):
                act.dma_start(par[:, j:j + 1], v).then_inc(s_small, 16)
            act.dma_start(w1s[:, :], w1).then_inc(s_small, 16)
            act.dma_start(w2s[:, :], w2).then_inc(s_small, 16)
            whole = N // P
            act.wait_ge(s_pro, 1)
            act.dma_start(xrow[:, 0:whole, :], x[0:whole * P, :].rearrange("(b p) h -> p b h", p=P))\
               .then_inc(s_xrow, 16)
            act.dma_start(xrow[0:N - whole * P, whole, :], x[whole * P:N, :]).then_inc(s_xrow, 16)
            act.wait_ge(s_xt, 16)
            act.wait_ge(s_pro, 2)
            act.activation(accT[:, 0:N], xT[:, :], ACT.Copy, scale=bn[:, 7:8]).then_inc(s_init, 1)

            def hidden(c, z):
                act.wait_ge(s_m1[z], c + 1)
                if c >= 2:
                    act.wait_ge(s_m2[z], c - 1)
                w = CHUNKS[c][1]
                act.activation(h1[:, c % 2, 0:w], ps[:, 4 + c % 2, 0:w], ACT.Relu, bias=b1s).then_inc(s_h1[z], 1)

            def second(c, z):
                act.wait_ge(s_m2[z], c + 1)
                c0, w = CHUNKS[c]
                act.activation(h2[:, c0:c0 + w], ps[:, 6 + c % 2, 0:w], ACT.Identity, bias=b2s)\
                   .then_inc(s_h2[z], 1)

            def part(q, which):
                if which:
                    act.wait_ge(s_rest, q + 1)
                else:
                    act.wait_ge(s_xrow, 32)
                a, b = PIECES[q][0], sum(PIECES[q])
                act.activation(x3[:, a:b, which, :], xrow[:, a:b, :], ACT.Copy).then_inc(s_part, 1)

            def iteration(i):
                first = isinstance(i, int) and i == 0
                for g in range(SLOTS):
                    n = i * SLOTS + g
                    if special(i) and g == SLOTS - 1:
                        act.wait_ge(s_got, (i - START) * NQ + NQ)
                        act.activation(got[:, 0, :], ps[:, 7, 2 * HID:3 * HID], ACT.Copy).then_inc(s_lo, 1)
                    act.wait_ge(s_pre, n + 1)
                    if not first or g >= 2:
                        act.wait_ge(s_win, n - 1)
                    act.activation(msg[:, g % 2, :, :], pre[:, g % 2, :, :], ACT.Relu).then_inc(s_msg, 1)
                    if isinstance(i, int) and i == START - 1:
                        if g < NQ:
                            part(g, 0)
                        if 1 <= g <= NQ:
                            part(g - 1, 1)
                    c = edge(i, g)
                    if c == 0:
                        act.wait_ge(s_small, 16 * 6)
                    if c is not None and c < EARLY:
                        hidden(c, 0)
                    if c:
                        second(c - 1, 0)

            run(act, iteration)
            act.wait_ge(s_pre, LASTG + 1)
            act.wait_ge(s_win, LASTG - 1)
            k = LASTG % 2
            act.activation(msg[:, k, 0:LASTT, :], pre[:, k, 0:LASTT, :], ACT.Relu).then_inc(s_msg, 1)
            act.activation(msg[0:REST, k, LASTT, :], pre[0:REST, k, LASTT, :], ACT.Relu).then_inc(s_msg, 1)

            act.wait_ge(s_flag, 2)
            redo = act.value_load(flag[0:1, 1:2], min_val=0, max_val=1)
            with act.If(redo > 0):
                for c in range(EARLY):
                    hidden(c, 1)
                    second(c, 1)
            for c in range(EARLY, len(CHUNKS)):
                hidden(c, 0)
                if c > EARLY:
                    second(c - 1, 0)
            second(len(CHUNKS) - 1, 0)
            act.wait_ge(s_bn, 1)
            act.activation(bn[:, 3:4], bn[:, 2:3], ACT.Sqrt).then_inc(s_sd, 1)
            act.wait_ge(s_bn, 2)
            def normed(n):
                b0, nb = BATCHES[n]
                a, b = b0 * P, min(N, (b0 + nb) * P)
                act.activation(accT[:, a:b], h2[:, a:b], ACT.Relu, scale=bn[:, 4:5], bias=bn[:, 6:7])\
                   .then_inc(s_relu, 1)

            normed(0)
            normed(1)
            for n, (b0, nb) in enumerate(BATCHES):
                if n + 2 < len(BATCHES):
                    normed(n + 2)
                act.wait_ge(s_ln, 2 * n + 1)
                act.activation(ln[:, 2, b0:b0 + nb], ln[:, 1, b0:b0 + nb], ACT.Sqrt).then_inc(s_lsd, 1)
                act.wait_ge(s_ln, 2 * n + 2)
                for b in range(b0, b0 + nb):
                    r = min(P, N - b * P)
                    last = act.activation(y[0:r, b, :], zt(b, r), ACT.Identity,
                                          scale=ln[0:r, 3, b:b + 1], bias=ln[0:r, 4, b:b + 1])
                last.then_inc(s_y, 1)

        @block.vector
        def _(dve):
            done = [0]

            def step(ins):
                done[0] += 1
                ins.then_inc(s_pro, 1)
                dve.wait_ge(s_pro, done[0])

            step(dve.memset(xrow[:, NBLK - 1, :], 0.0))
            for h in range(2):
                dve.memset(ea[h][EDIM:K, :], 1.0)
            dve.wait_ge(s_we, 16 * 3)
            step(dve.tensor_scalar_add(bn[:, 7:8], eps1, 1.0))
            dve.memset(accT[:, N:N + WIN], 0.0).then_inc(s_init, 1)
            dve.memset(ones[:, :], 1.0)
            dve.memset(lnst[:, NBLK - 1, :], 0.0)
            dve.memset(leastT[:, :], 0.0)
            dve.wait_ge(s_dst, 32)
            step(dve.memset(least[:, LASTG:GROUPS], float(N)))
            dve.tensor_copy(rel[0:REST, FULL:FULL + 1], dsti[0:REST, FULL:FULL + 1])
            step(dve.tensor_copy(rel[:, 0:FULL], dsti[:, 0:FULL]))
            dve.tensor_reduce(least[:, 0:LOOPED], rel[:, 0:LOOPED * GROUP].rearrange("p (g t) -> p g t", t=GROUP),
                              AX.X, ALU.min)
            if LASTT:
                step(dve.tensor_reduce(least[:, LASTG:GROUPS], rel[:, LOOPED * GROUP:FULL], AX.X, ALU.min))
            step(dve.tensor_tensor(least[0:REST, LASTG:GROUPS], least[0:REST, LASTG:GROUPS],
                                   rel[0:REST, FULL:FULL + 1], ALU.min))
            dve.nop().then_inc(s_tr, 1)
            dve.wait_ge(s_tr, 2)
            for b in range(GBLK):
                w = min(P, GROUPS - b * P)
                last = dve.tensor_reduce(leastT[0:w, b:b + 1], ps[0:w, b, 0:P], AX.X, ALU.min)
            step(last)
            dve.wait_ge(s_const, 4)
            for b in range(GBLK):
                last = dve.tensor_scalar(diag[:, b, :], ident[:, :], leastT[:, b:b + 1], None, ALU.mult)
            last.then_inc(s_tr, 1)
            dve.wait_ge(s_tr, 4)
            step(dve.tensor_copy(base[:, :], ps[:, 4, 0:GROUPS]))
            dve.tensor_copy(basei[:, :], base[:, :])
            dve.tensor_copy(iota[:, :], iota_i[:, :])
            v = rel[:, 0:LOOPED * GROUP].rearrange("p (g t) -> p g t", t=GROUP)
            dve.tensor_tensor(v, v, base[:, 0:LOOPED].unsqueeze(2).to_broadcast([P, LOOPED, GROUP]), ALU.subtract)
            if LASTT:
                dve.tensor_scalar(rel[:, LOOPED * GROUP:FULL], rel[:, LOOPED * GROUP:FULL],
                                  base[:, LASTG:GROUPS], None, ALU.subtract)
            step(dve.tensor_scalar(rel[0:REST, FULL:FULL + 1], rel[0:REST, FULL:FULL + 1],
                                   base[0:REST, LASTG:GROUPS], None, ALU.subtract))
            step(dve.tensor_reduce(over[:, 0:1], rel[:, 0:FULL], AX.X, ALU.max))
            step(dve.tensor_tensor(over[0:REST, 0:1], over[0:REST, 0:1], rel[0:REST, FULL:FULL + 1], ALU.max))
            dve.nop().then_inc(s_tr, 1)
            dve.wait_ge(s_tr, 6)
            step(dve.tensor_reduce(overT[0:1, 0:1], ps[0:1, 5, 0:P], AX.X, ALU.max))
            step(dve.tensor_scalar(flagf[0:1, 0:1], overT[0:1, 0:1], float(WIN), None, ALU.is_ge))
            dve.tensor_copy(flag[0:1, 0:1], flagf[0:1, 0:1]).then_inc(s_flag, 1)
            step(dve.tensor_reduce(flagf[0:1, 1:2], base[0:1, (ITERS - AHEAD) * SLOTS:GROUPS], AX.X, ALU.min))
            step(dve.tensor_scalar(flagf[0:1, 2:3], flagf[0:1, 1:2], float(EARLY_N), None, ALU.is_lt))
            step(dve.tensor_tensor(flagf[0:1, 3:4], flagf[0:1, 2:3], flagf[0:1, 0:1], ALU.max))
            dve.tensor_copy(flag[0:1, 1:2], flagf[0:1, 3:4]).then_inc(s_flag, 1)
            dve.nop().then_inc(s_tr, 1)

            def one_hot(n, k, first):
                if not first:
                    dve.wait_ge(s_win, n - 1)
                t0 = n * GROUP
                dve.tensor_tensor(
                    hot[:, k, :, :],
                    rel[:, bass.ds(t0, GROUP)].unsqueeze(2).to_broadcast([P, GROUP, WIN]),
                    iota[:, :].unsqueeze(1).to_broadcast([P, GROUP, WIN]), ALU.is_equal).then_inc(s_hot, 1)

            def add_x(i, g, n, first):
                dve.wait_ge(s_lin, n + 1)
                dve.wait_ge(s_xg[g], gathered(i, g))
                if not first:
                    dve.wait_ge(s_msg, n - 1)
                if not (special(i) and g == SLOTS - 1):
                    dve.tensor_tensor(pre[:, g % 2, :, :], ps_lin(g % 2), xg[:, g, :, :], ALU.add)\
                       .then_inc(s_pre, 1)
                    return
                G = GROUP - 1
                dve.wait_ge(s_lo, (i - START) + 1)
                dve.tensor_tensor(got[:, 1, :], ps[:, 7, HID:2 * HID], got[:, 0, :], ALU.add).then_inc(s_dve, 1)
                dve.tensor_tensor(pre[:, g % 2, 0:G, :], ps_lin(g % 2)[:, 0:G, :], xg[:, g, 0:G, :], ALU.add)
                dve.wait_ge(s_dve, (i - START) * 2 + 1)
                dve.tensor_tensor(got[:, 2, :], ps[:, 7, 0:HID], got[:, 1, :], ALU.add).then_inc(s_dve, 1)
                dve.wait_ge(s_dve, (i - START) * 2 + 2)
                dve.tensor_tensor(pre[:, g % 2, G, :], ps_lin(g % 2)[:, G, :], got[:, 2, :], ALU.add)\
                   .then_inc(s_pre, 1)

            def select(i, q):
                if q == 0:
                    dve.wait_ge(s_srcb, (i - START) * 16 + 16)
                if not isinstance(i, int) or q >= 2:
                    dve.wait_ge(s_got, (i - START) * NQ + max(q - 1, 0))
                b0, nb = PIECES[q]
                dve.tensor_tensor(sel[:, q % 2, 0:nb, :], srcb[:, :].unsqueeze(1).to_broadcast([P, nb, P]),
                                  node[:, b0:b0 + nb].unsqueeze(2).to_broadcast([P, nb, P]), ALU.is_equal)\
                   .then_inc(s_sel, 1)

            def remains(q, which):
                a, b = PIECES[q][0], sum(PIECES[q])
                dve.wait_ge(s_part, max(2 * q, 1) if which == 0 else min(2 * q + 3, 2 * NQ))
                to = xrow[:, a:b, :] if which == 0 else x3[:, a:b, 2, :]
                dve.tensor_tensor(to, xrow[:, a:b, :], x3[:, a:b, which, :], ALU.subtract).then_inc(s_rest, 1)

            def add_window(n, k, first=False):
                at = dve.value_load(basei[0:1, bass.ds(n, 1)], min_val=0, max_val=N - 1)
                dve.wait_ge(s_win, n + 1)
                if not first:
                    dve.wait_ge(s_acc, n)
                dve.tensor_tensor(accT[:, bass.ds(at, WIN)], accT[:, bass.ds(at, WIN)], ps_win(k), ALU.add)\
                   .then_inc(s_acc, 1)

            def iteration(i):
                first = isinstance(i, int) and i == 0
                for g in range(SLOTS):
                    n = i * SLOTS + g
                    one_hot(n, g % 2, first and g < 2)
                    if special(i) and g < NQ:
                        select(i, g)
                    add_x(i, g, n, first and g < 2)
                    if not first or g >= 1:
                        if first and g == 1:
                            dve.wait_ge(s_init, 2)
                        add_window(n - 1, (g - 1) % 2, first and g == 1)
                    if isinstance(i, int) and i == START - 1:
                        if g < NQ:
                            remains(g, 0)
                        if g == NQ:
                            for q in range(NQ):
                                remains(q, 1)
                    c = edge(i, g)
                    if c is not None and c >= 2:
                        stats(c - 2, 0)

            def stats(c, z):
                c0, w = CHUNKS[c]
                dve.wait_ge(s_h2[z], c + 1)
                dve.bn_stats(bnst[:, c, :], h2[:, c0:c0 + w]).then_inc(s_st, 1)

            run(dve, iteration)
            stats(EARLY - 1, 0)
            n, k = LASTG, LASTG % 2
            dve.wait_ge(s_win, n - 1)
            for j, r in LAST:
                last = dve.tensor_scalar(hot[0:r, k, j, :], iota[0:r, :], rel[0:r, LOOPED * GROUP + j:LOOPED * GROUP + j + 1],
                                         None, ALU.is_equal)
            last.then_inc(s_hot, 1)
            dve.wait_ge(s_lin, n + 1)
            dve.wait_ge(s_xg[0], gathered(ITERS - 1, 0) + 16 * len(LAST))
            dve.wait_ge(s_msg, n - 1)
            for j, r in LAST:
                last = dve.tensor_tensor(pre[0:r, k, j, :], ps_lin(k)[0:r, j, :], xg[0:r, 0, j, :], ALU.add)
            last.then_inc(s_pre, 1)
            add_window(n - 1, (n - 1) % 2)
            add_window(n, k)
            dve.wait_ge(s_acc, GROUPS)

            many = dve.value_load(flag[0:1, 0:1], min_val=0, max_val=1)
            with dve.If(many > 0):
                dve.memset(g_ea[EDIM:K, :], 1.0).then_inc(g_const, 1)
                dve.wait_ge(g_const, 2)
                dve.tensor_copy(iota_all[:, 0:N], iota_all[:, 0:N].bitcast(i32)).then_inc(g_const, 1)
                dve.wait_ge(g_const, 3)
                STEPS = 8

                def tile(t, g, r, n):
                    def wait(k):
                        dve.wait_ge(g_vec, n * STEPS + k)
                    dve.tensor_scalar(g_dst[0:r, 0:1], rel[0:r, bass.ds(t, 1)], float(WIN), None, ALU.is_ge)\
                       .then_inc(g_vec, 1)
                    dve.tensor_scalar(g_dst[0:r, 1:2], rel[0:r, bass.ds(t, 1)], base[0:r, bass.ds(g, 1)], 1.0,
                                      ALU.add, ALU.add).then_inc(g_vec, 1)
                    wait(2)
                    dve.tensor_tensor(g_dst[0:r, 2:3], g_dst[0:r, 0:1], g_dst[0:r, 1:2], ALU.mult).then_inc(g_vec, 1)
                    wait(3)
                    dve.tensor_scalar_add(g_dst[0:r, 3:4], g_dst[0:r, 2:3], -1.0).then_inc(g_vec, 1)
                    wait(4)
                    dve.tensor_scalar(hot_all[0:r, :], iota_all[0:r, 0:N], g_dst[0:r, 3:4], None, ALU.is_equal)
                    dve.wait_ge(g_lin, n + 1)
                    dve.wait_ge(g_gat, (n + 1) * 16)
                    dve.tensor_tensor(g_msg[0:r, :], ps[0:r, 7, 0:HID], g_xg[0:r, :], ALU.add).then_inc(g_vec, 1)
                    wait(5)
                    dve.tensor_scalar_max(g_msg[0:r, :], g_msg[0:r, :], 0.0).then_inc(g_vec, 1)
                    for m, (a, b) in enumerate(SPLIT):
                        dve.wait_ge(g_sum, n * len(SPLIT) + m + 1)
                        c0, c1 = a * BANK, min(N, b * BANK)
                        dve.tensor_tensor(accT[:, c0:c1], accT[:, c0:c1],
                                          ps[:, 0:b - a, :].rearrange("p a n -> p (a n)")[:, 0:c1 - c0], ALU.add)\
                           .then_inc(g_vec, 1)
                    wait(STEPS)

                with dve.Fori(0, LOOPED) as g:
                    for j in range(GROUP):
                        tile(g * GROUP + j, g, P, g * GROUP + j)
                for j, r in LAST:
                    tile(LOOPED * GROUP + j, LASTG, r, LOOPED * GROUP + j)
            dve.nop().then_inc(s_agg, 1)

            redo = dve.value_load(flag[0:1, 1:2], min_val=0, max_val=1)
            with dve.If(redo > 0):
                for c, (c0, w) in enumerate(CHUNKS[0:EARLY]):
                    dve.wait_ge(s_h2[1], c + 1)
                    last = dve.bn_stats(bnst[:, c, :], h2[:, c0:c0 + w])
                last.then_inc(s_redone, 1)
                dve.wait_ge(s_redone, 1)
            for c in range(EARLY, len(CHUNKS)):
                stats(c, 0)
            dve.wait_ge(s_st, len(CHUNKS))
            done[0] = len(CHUNKS)

            def stat(ins):
                done[0] += 1
                ins.then_inc(s_st, 1)
                dve.wait_ge(s_st, done[0])

            stat(dve.bn_aggr(bn[:, 0:2], bnst[:, :, :].rearrange("p a b -> p (a b)")))
            dve.tensor_scalar_add(bn[:, 2:3], bn[:, 1:2], BN_EPS).then_inc(s_bn, 1)
            dve.wait_ge(s_sd, 1)
            stat(dve.reciprocal(bn[:, 5:6], bn[:, 3:4]))
            stat(dve.tensor_tensor(bn[:, 4:5], bn[:, 5:6], gms, ALU.mult))
            stat(dve.tensor_tensor(bn[:, 2:3], bn[:, 4:5], bn[:, 0:1], ALU.mult))
            dve.tensor_tensor(bn[:, 6:7], bts, bn[:, 2:3], ALU.subtract).then_inc(s_bn, 1)

            def residual(n):
                b0, nb = BATCHES[n]
                a, b = b0 * P, min(N, (b0 + nb) * P)
                dve.wait_ge(s_relu, n + 1)
                dve.scalar_tensor_tensor(out=accT[:, a:b], in0=xT[:, a:b], scalar=2.0, in1=accT[:, a:b],
                                         op0=ALU.mult, op1=ALU.add).then_inc(s_z, 1)

            residual(0)
            for n, (b0, nb) in enumerate(BATCHES):
                if n + 1 < len(BATCHES):
                    residual(n + 1)
                dve.wait_ge(s_zt, n + 1)
                for b in range(b0, b0 + nb):
                    r = min(P, N - b * P)
                    last = dve.bn_stats(lnst[0:r, b, :], zt(b, r))
                stat(last)
                me, qe, mo, qo = (lnst[:, b0:b0 + nb, j] for j in (1, 2, 4, 5))
                m, v, t, u, w = (ln[:, j, b0:b0 + nb] for j in (0, 1, 5, 3, 4))
                dve.tensor_tensor(m, me, mo, ALU.add)
                dve.tensor_tensor(t, me, mo, ALU.subtract)
                stat(dve.tensor_tensor(v, qe, qo, ALU.add))
                stat(dve.scalar_tensor_tensor(out=t, in0=t, scalar=0.25, in1=t, op0=ALU.mult, op1=ALU.mult))
                stat(dve.scalar_tensor_tensor(out=v, in0=v, scalar=1.0 / HID, in1=t, op0=ALU.mult, op1=ALU.add))
                stat(dve.tensor_scalar_add(v, v, LN_EPS))
                dve.nop().then_inc(s_ln, 1)
                dve.wait_ge(s_lsd, n + 1)
                stat(dve.reciprocal(u, ln[:, 2, b0:b0 + nb]))
                dve.scalar_tensor_tensor(out=w, in0=m, scalar=-0.5, in1=u, op0=ALU.mult, op1=ALU.mult)\
                   .then_inc(s_ln, 1)

        @block.tensor
        def _(pe):
            pe.wait_ge(s_const, 4)
            pe.wait_ge(s_tr, 1)
            for b in range(GBLK):
                w = min(P, GROUPS - b * P)
                last = pe.transpose(ps[0:w, b, 0:P], least[:, b * P:b * P + w], ident[:, :])
            last.then_inc(s_tr, 1)
            pe.wait_ge(s_tr, 3)
            for b in range(GBLK):
                w = min(P, GROUPS - b * P)
                last = pe.matmul(ps[:, 4, b * P:b * P + w], ones[:, :], diag[:, b, 0:w], start=True, stop=True)
            last.then_inc(s_tr, 1)
            pe.wait_ge(s_tr, 5)
            pe.transpose(ps[0:1, 5, 0:P], over[:, 0:1], ident[:, :]).then_inc(s_tr, 1)
            pe.wait_ge(s_we, 16 * 3)
            pe.wait_ge(s_tr, 7)

            def linear(h, at, k, tiles):
                for j, r in tiles:
                    last = pe.matmul(ps_lin(k)[0:r, j, :], ea[h][:, (at + j) * P:(at + j) * P + r], wea[:, :],
                                     start=True, stop=True)
                last.then_inc(s_lin, 1)

            def window(k, tiles):
                for j, r in tiles:
                    last = pe.matmul(ps_win(k), msg[0:r, k, j, :], hot[0:r, k, j, :],
                                     start=(j == 0), stop=(j == len(tiles) - 1))
                last.then_inc(s_win, 1)

            ALL = [(j, P) for j in range(GROUP)]

            def window_of(n, k, first):
                pe.wait_ge(s_msg, n + 1)
                pe.wait_ge(s_hot, n + 1)
                if not first:
                    pe.wait_ge(s_acc, n - 1)
                window(k, ALL)

            def gather(i, q):
                pe.wait_ge(s_sel, (i - START) * NQ + (q + 1))
                if q == 0:
                    pe.wait_ge(s_rest, 2 * NQ)
                    if not isinstance(i, int):
                        pe.wait_ge(s_pre, i * SLOTS)
                b0, nb = PIECES[q]
                for b in range(nb):
                    last = pe.matmul(ps[:, 7, 0:3 * HID], sel[:, q % 2, b, :],
                                     x3[:, b0 + b, :, :].rearrange("p a h -> p (a h)"),
                                     start=(b0 + b == 0), stop=(b0 + b == NBLK - 1))
                last.then_inc(s_got, 1)

            def iteration(i):
                first = isinstance(i, int) and i == 0
                for g in range(SLOTS):
                    n = i * SLOTS + g
                    h, at = divmod(g * GROUP, HALF)
                    if at == 0:
                        pe.wait_ge(s_ea[h], (i + 1) * 16)
                    if not first or g >= 2:
                        pe.wait_ge(s_pre, n - 1)
                    linear(h, at, g % 2, ALL)
                    if not first or g >= 1:
                        window_of(n - 1, (g - 1) % 2, first and g < 3)
                    if special(i) and g < NQ:
                        gather(i, g)
                    c = edge(i, g)
                    if c == 0:
                        pe.wait_ge(s_small, 16 * 6)
                        pe.wait_ge(s_acc, (ITERS - AHEAD) * SLOTS)
                    if c is not None and c < EARLY:
                        first_product(c, 0)
                    if c:
                        second_product(c - 1, 0)

            def first_product(c, z):
                c0, w = CHUNKS[c]
                if c >= 2:
                    pe.wait_ge(s_h1[z], c - 1)
                pe.matmul(ps[:, 4 + c % 2, 0:w], w1s[:, :], accT[:, c0:c0 + w], start=True, stop=True)\
                  .then_inc(s_m1[z], 1)

            def second_product(c, z):
                w = CHUNKS[c][1]
                pe.wait_ge(s_h1[z], c + 1)
                if c >= 2:
                    pe.wait_ge(s_h2[z], c - 1)
                pe.matmul(ps[:, 6 + c % 2, 0:w], w2s[:, :], h1[:, c % 2, 0:w], start=True, stop=True)\
                  .then_inc(s_m2[z], 1)

            run(pe, iteration)
            pe.wait_ge(s_ea[0], (ITERS + 1) * 16)
            pe.wait_ge(s_pre, LASTG - 1)
            linear(0, 0, LASTG % 2, LAST)
            window_of(LASTG - 1, (LASTG - 1) % 2, False)
            pe.wait_ge(s_msg, LASTG + 2)
            pe.wait_ge(s_hot, LASTG + 1)
            pe.wait_ge(s_acc, LASTG - 1)
            window(LASTG % 2, LAST)

            pe.wait_ge(s_flag, 1)
            many = pe.value_load(flag[0:1, 0:1], min_val=0, max_val=1)
            with pe.If(many > 0):
                pe.wait_ge(g_const, 3)
                pe.wait_ge(s_h2[0], EARLY)
                STEPS = 8

                def tile(r, n, first):
                    pe.wait_ge(g_load, (n + 1) * 32)
                    if not first:
                        pe.wait_ge(g_vec, n * STEPS)
                    pe.matmul(ps[0:r, 7, 0:HID], g_ea[:, 0:r], wea[:, :], start=True, stop=True).then_inc(g_lin, 1)
                    pe.wait_ge(g_vec, n * STEPS + 6)
                    for m, (a, b) in enumerate(SPLIT):
                        if m:
                            pe.wait_ge(g_vec, n * STEPS + 6 + m)
                        for q in range(a, b):
                            w = min(BANK, N - q * BANK)
                            last = pe.matmul(ps[:, q - a, 0:w], g_msg[0:r, :], hot_all[0:r, q * BANK:q * BANK + w],
                                             start=True, stop=True)
                        last.then_inc(g_sum, 1)

                tile(P, 0, True)
                with pe.Fori(1, FULL) as t:
                    tile(P, t, False)
                tile(REST, FULL, False)

            pe.wait_ge(s_agg, 1)
            pe.wait_ge(s_flag, 2)
            redo = pe.value_load(flag[0:1, 1:2], min_val=0, max_val=1)
            with pe.If(redo > 0):
                pe.wait_ge(s_h2[0], EARLY)
                for c in range(EARLY):
                    first_product(c, 1)
                    second_product(c, 1)
                pe.wait_ge(s_h2[1], EARLY)
            for c in range(EARLY, len(CHUNKS)):
                first_product(c, 0)
                if c > EARLY:
                    second_product(c - 1, 0)
            second_product(len(CHUNKS) - 1, 0)
            pe.wait_ge(s_h2[0], len(CHUNKS))
            for n, (b0, nb) in enumerate(BATCHES):
                pe.wait_ge(s_z, n + 1)
                used = [m + 1 for m, (c0, cb) in enumerate(BATCHES) if c0 < (b0 + nb + 3) // 4 * 4 - 32]
                if used:
                    pe.wait_ge(s_y, used[-1])
                for b in range(b0, b0 + nb):
                    r = min(P, N - b * P)
                    last = pe.transpose(zt(b, r), accT[:, b * P:b * P + r], ident[:, :])
                last.then_inc(s_zt, 1)


def kernel(**inputs):
    import numpy as _np
    import concourse.bacc as _bacc
    from concourse import mybir as _mybir
    from concourse.bass_utils import run_bass_kernel_spmd as _run

    P, HALF = 128, 12
    a = {k: _np.asarray(v) for k, v in inputs.items()}
    x, src, dst, ea = a["x"], a["src"], a["dst"], a["edge_attr_64"]
    E = src.shape[0]
    full = E // P
    halves = full // (2 * HALF) * 2
    col = lambda v: v.reshape(-1, 1)
    data = {
        "x": x,
        "xt": x.T,
        "src_loop": src[:halves * HALF * P].reshape(halves, HALF, P).transpose(0, 2, 1),
        "src_row": src.reshape(1, -1),
        "src_col": col(src),
        "dst_tiles": dst[:full * P].reshape(full, P).T,
        "dst_last": col(dst[full * P:]),
        "eat": ea.T,
        "we": a["L0_gnn_We"],
        "be": a["L0_gnn_be"].reshape(1, -1),
        "w1": a["L0_gnn_W1"],
        "b1": col(a["L0_gnn_b1"]),
        "w2": a["L0_gnn_W2"],
        "b2": col(a["L0_gnn_b2"]),
        "gamma": col(a["L0_gnn_gamma"]),
        "beta": col(a["L0_gnn_beta"]),
        "eps": a["L0_gnn_eps"].reshape(1, 1),
    }
    nc = _bacc.Bacc("TRN2", target_bir_lowering=False, num_devices=1)
    arrays, args = {}, []
    for name, v in data.items():
        v = _np.ascontiguousarray(v)
        arrays[f"in_{name}"] = v
        args.append(nc.dram_tensor(f"in_{name}", v.shape, _mybir.dt.from_np(v.dtype), kind="ExternalInput").ap())
    args.append(nc.dram_tensor("out", x.shape, _mybir.dt.float32, kind="ExternalOutput").ap())
    gine_layer_kernel(nc, *args)
    r = _run(nc, [arrays], core_ids=[0])
    return r.results[0]["out"]
```

```python
import concourse.bass as bass
from concourse import mybir
from contextlib import ExitStack


def gine_layer_kernel(
    nc: bass.Bass,
    x: bass.AP,
    xt: bass.AP,
    src_loop: bass.AP,
    src_row: bass.AP,
    src_col: bass.AP,
    dst_tiles: bass.AP,
    dst_last: bass.AP,
    eat: bass.AP,
    we: bass.AP,
    be: bass.AP,
    w1: bass.AP,
    b1: bass.AP,
    w2: bass.AP,
    b2: bass.AP,
    gamma: bass.AP,
    beta: bass.AP,
    eps: bass.AP,
    out: bass.AP,
):
    fp32 = mybir.dt.float32
    i32 = mybir.dt.int32
    bf16 = mybir.dt.bfloat16
    ALU = mybir.AluOpType
    ACT = mybir.ActivationFunctionType
    AX = mybir.AxisListType

    P = 128
    N, HID = x.shape
    EDIM, E = eat.shape
    K = EDIM + 1
    EPS = 1e-5

    GROUP = 4
    WIN = 64
    SPAN = src_loop.shape[2] // GROUP
    PARTS = 2
    SLOTS = SPAN * PARTS
    TILES = SPAN * GROUP
    ITERS = src_loop.shape[0] // PARTS
    FULL = E // P
    REST = E - FULL * P
    GE = GROUP * P
    LOOPED = ITERS * SLOTS
    LASTT = FULL - LOOPED * GROUP
    GROUPS = LOOPED + 1
    LASTG = LOOPED
    assert 0 <= LASTT < GROUP and REST > 0

    NBLK = -(-N // P)
    GBLK = -(-GROUPS // P)
    START = 1
    PIECE = -(-NBLK // (SPAN - 1))
    PIECES = [(b, min(PIECE, NBLK - b)) for b in range(0, NBLK, PIECE)]
    NQ = len(PIECES)
    AHEAD = 1
    CH = 484
    EARLY = 12
    EARLY_N = EARLY * CH
    TAIL = (N - EARLY_N) // 4 * 2
    CHUNKS = [(c * CH, CH) for c in range(EARLY)] + [(EARLY_N, TAIL), (EARLY_N + TAIL, N - EARLY_N - TAIL)]
    BATCHES = [(0, 4), (4, 8), (12, 8), (20, 8), (28, 8), (36, 8), (44, 5)]
    BY_ACT = 4
    assert BATCHES[-1][0] + BATCHES[-1][1] == NBLK and SPAN >= 4

    BANK = 512
    WALL = -(-N // BANK)
    SPLIT = [(0, 7), (7, WALL)]

    ctx = ExitStack()
    with ctx:
        def sb(name, shape, dt=fp32):
            return ctx.enter_context(nc.sbuf_tensor(name, shape, dt))

        def sem(name):
            return ctx.enter_context(nc.semaphore(name))

        accT = sb("accT", [HID, N + WIN])
        xT = sb("xT", [HID, N])
        ea = [sb(f"ea{h}", [K, TILES * P]) for h in range(PARTS)]
        xg = sb("xg", [P, SLOTS, GROUP, HID])
        msg = sb("msg", [P, 2, GROUP, HID])
        hot = sb("hot", [P, 2, GROUP, WIN])
        idxb = [sb(f"idxb{h}", [P, TILES], i32) for h in range(PARTS)]
        idx_last = sb("idx_last", [P, GROUP], i32)
        rel = sb("rel", [P, FULL + 1])
        base = sb("base", [P, GROUPS])
        basei = sb("basei", [P, GROUPS], i32)
        over = sb("over", [P, 2])
        overT = sb("overT", [1, 1])
        flag = sb("flag", [1, 2], i32)
        flagf = sb("flagf", [1, 4])
        iota_i = sb("iota_i", [P, WIN], i32)
        ident = sb("ident", [P, P])
        epsc = sb("epsc", [P, 2])
        ones = sb("ones", [P, P])
        wea = sb("wea", [K, HID])
        w1s = sb("w1s", [HID, HID])
        w2s = sb("w2s", [HID, HID])
        par = sb("par", [HID, 5])
        b1s, b2s, gms, bts, eps1 = (par[:, j:j + 1] for j in range(5))
        x3 = sb("x3", [P, NBLK, 3, HID], bf16)
        node = sb("node", [P, NBLK], i32)
        srcb = [sb(f"srcb{h}", [P, P], i32) for h in range(PARTS)]
        sel = sb("sel", [P, 2, PIECE, P], bf16)
        got = sb("got", [P, 3, HID])
        bnst = sb("bnst", [HID, len(CHUNKS), 6])
        bn = sb("bn", [HID, 8])
        bn_mean, bn_var, bn_sd, bn_inv, bn_scale, bn_prod, bn_shift, eps_plus1 = (bn[:, j:j + 1] for j in range(8))
        lnst = sb("lnst", [P, NBLK, 6])
        ln = sb("ln", [P, 6, NBLK])
        MEAN2, VAR, DEV, INV, SHIFT, TEMP = range(6)
        hot_all = sb("hot_all", [P, N])
        iota_all = sb("iota_all", [P, NBLK * HID])
        h2 = hot_all
        y = iota_all[:, :].rearrange("p (b h) -> p b h", h=HID)
        xrow = y
        h1 = iota_all[:, 0:2 * BANK].rearrange("p (k n) -> p k n", k=2)
        dsti = hot_all[:, 0:FULL + 1].bitcast(i32)
        least = hot_all[:, FULL + 1:FULL + 1 + GROUPS]
        leastT = hot_all[:, FULL + 1 + GROUPS:FULL + 1 + GROUPS + GBLK]
        diag = hot_all[:, 2048:2048 + GBLK * P].rearrange("p (b n) -> p b n", n=P)
        assert FULL + 1 + GROUPS + GBLK <= 2048
        g_idx = sb("g_idx", [P, 1], i32)
        g_ea = sb("g_ea", [K, P])
        g_xg = sb("g_xg", [P, HID])
        g_msg = sb("g_msg", [P, HID])
        g_dst = sb("g_dst", [P, 4])

        ps = ctx.enter_context(nc.psum_tensor("ps", [P, 8, BANK], fp32))
        iota = ps[:, 6, 0:WIN]
        nodes = ps[:, 6, WIN:WIN + NBLK]

        def ps_lin(k):
            return ps[:, k, :].rearrange("p (t n) -> p t n", t=GROUP)

        def ps_win(k):
            return ps[:, 2 + k, 0:WIN]

        s_xrow = sem("s_xrow")
        s_part = [sem("s_hi"), sem("s_mid")]
        s_rest = [sem("s_rest"), sem("s_least")]
        s_srcb = [sem(f"s_srcb{h}") for h in range(PARTS)]
        s_sel = sem("s_sel")
        s_got = sem("s_got")
        s_lo = sem("s_lo")
        s_join = sem("s_join")
        s_const = sem("s_const")
        s_apart = sem("s_apart")
        s_small = sem("s_small")
        s_dst = sem("s_dst")
        s_xt = sem("s_xt")
        s_ea = [sem(f"s_ea{h}") for h in range(PARTS)]
        s_idx = [sem(f"s_idx{h}") for h in range(PARTS)]
        s_xg = [sem(f"s_xg{g}") for g in range(SLOTS)]
        s_last = sem("s_last")
        s_pro = sem("s_pro")
        s_tr = sem("s_tr")
        s_we = sem("s_we")
        s_x2 = sem("s_x2")
        s_init = sem("s_init")
        s_lin = sem("s_lin")
        s_pre = sem("s_pre")
        s_msg = sem("s_msg")
        s_hot = sem("s_hot")
        s_win = sem("s_win")
        s_acc = sem("s_acc")
        s_flag = sem("s_flag")
        g_const = sem("g_const")
        g_load = sem("g_load")
        g_gat = sem("g_gat")
        g_lin = sem("g_lin")
        g_vec = sem("g_vec")
        g_sum = sem("g_sum")
        s_m1 = [sem("s_m1"), sem("r_m1")]
        s_h1 = [sem("s_h1"), sem("r_h1")]
        s_m2 = [sem("s_m2"), sem("r_m2")]
        s_h2 = [sem("s_h2"), sem("r_h2")]
        s_redone = sem("s_redone")
        s_st = sem("s_st")
        s_bn = sem("s_bn")
        s_sd = sem("s_sd")
        s_relu = [sem("s_relu"), sem("s_relu_pool")]
        s_lift = sem("s_lift")
        s_zt = sem("s_zt")
        s_stat = sem("s_stat")
        s_var = sem("s_var")
        s_lsd = sem("s_lsd")
        s_inv = sem("s_inv")
        s_shift = sem("s_shift")
        s_y = [sem(f"s_y{n}") for n in range(len(BATCHES))]
        s_out = sem("s_out")

        block = ctx.enter_context(nc.Block())

        def wait_apart(eng, semaphore, value):
            eng.wait_ge(semaphore, value)
            eng.sem_inc(s_apart, 1)

        LAST = [(j, P) for j in range(LASTT)] + [(LASTT, REST)]
        LAST_E0 = LASTG * GE

        def spans(i):
            return not isinstance(i, int) or START <= i < ITERS - AHEAD

        def special(i, g):
            return g % SPAN == SPAN - 1 and spans(i)

        def span(i, g):
            return (i - START) * PARTS + g // SPAN

        def gathered(i, g):
            if special(i, g):
                return i * (16 * (GROUP - 1)) + 16 * (GROUP - 1 + START)
            if g % SPAN == SPAN - 1 and i >= START:
                return (i + 1) * (16 * GROUP) - 16 * (ITERS - AHEAD - START)
            return (i + 1) * (16 * GROUP)

        def before(i, g):
            if isinstance(i, int):
                return gathered(i - 1, g)
            if special(i, g):
                return i * (16 * (GROUP - 1)) + 16 * START
            return i * (16 * GROUP)

        def run(eng, iteration, between=None):
            for i in range(START + 1):
                iteration(i)
            with eng.Fori(START + 1, ITERS - AHEAD - 1) as i:
                iteration(i)
            held = between() if between else None
            for i in range(ITERS - AHEAD - 1, ITERS):
                iteration(i)
            return held

        def flags(eng):
            eng.wait_ge(s_flag, 2)
            return (eng.value_load(flag[0:1, 0:1], min_val=0, max_val=1),
                    eng.value_load(flag[0:1, 1:2], min_val=0, max_val=1))

        def early(i, g):
            if not isinstance(i, int) or i < ITERS - AHEAD:
                return []
            at = (i - (ITERS - AHEAD)) * SLOTS + g
            return [c for c in range(EARLY) if c * (AHEAD * SLOTS) // EARLY == at]

        LATE = (ITERS - AHEAD) * SLOTS - 2

        def bank1(c):
            return 4 if c < EARLY else 4 + c % 2

        def bank2(c):
            return 5 if c < EARLY else 6 + c % 2

        def shared(n):
            return (0, 0, 4, 0, 4, 4, 1)[n]

        def zt(b, rows):
            return ps[0:rows, b // 4 % 8, b % 4 * P:(b % 4 + 1) * P]

        @block.sync
        def _(sp):
            def load_part(i, h):
                sp.dma_start(idxb[h][:, :], src_loop[PARTS * i + h]).then_inc(s_idx[h], 16)
                sp.dma_start(ea[h][0:EDIM, :], eat[:, bass.ds((PARTS * i + h) * (TILES * P), TILES * P)])\
                  .then_inc(s_ea[h], 16)

            def load_srcb(i, h):
                tile = (i * PARTS + h) * TILES + (TILES - 1)
                sp.dma_start(srcb[h][:, :], src_row[:, bass.ds(tile * P, P)].partition_broadcast(P))\
                  .then_inc(s_srcb[h], 16)

            sp.dma_start(idxb[0][:, :], src_loop[0]).then_inc(s_idx[0], 16)
            sp.dma_start(dsti[:, 0:FULL], dst_tiles).then_inc(s_dst, 16)
            sp.dma_start(dsti[0:REST, FULL:FULL + 1], dst_last).then_inc(s_dst, 16)
            sp.dma_start(ea[0][0:EDIM, :], eat[:, 0:TILES * P]).then_inc(s_ea[0], 16)
            load_part(0, 1)
            for j, r in LAST:
                e0 = LAST_E0 + j * P
                sp.dma_start(idx_last[0:r, j:j + 1], src_col[e0:e0 + r, :]).then_inc(s_last, 16)

            def iteration(i):
                if isinstance(i, int) and i == 0:
                    return
                for h in range(PARTS):
                    for g in range(h * SPAN, (h + 1) * SPAN):
                        wait_apart(sp, s_xg[g], before(i, g))
                    wait_apart(sp, s_lin, (i - 1) * SLOTS + (h + 1) * SPAN)
                    load_part(i, h)
                    if spans(i):
                        if not isinstance(i, int) or i > START:
                            wait_apart(sp, s_sel, (span(i - 1, h * SPAN) + 1) * NQ)
                        load_srcb(i, h)

            run(sp, iteration)
            sp.wait_ge(s_lin, (ITERS - 1) * SLOTS + SPAN)
            sp.dma_start(ea[0][0:EDIM, 0:E - LAST_E0], eat[:, LAST_E0:E]).then_inc(s_ea[0], 16)

            sp.wait_ge(s_flag, 1)
            general = sp.value_load(flag[0:1, 0:1], min_val=0, max_val=1)
            with sp.If(general > 0):
                def tile(t, r, n):
                    wait_apart(sp, g_sum, n * len(SPLIT))
                    sp.dma_start(g_idx[0:r, :], src_col[bass.ds(t * P, r), :]).then_inc(g_load, 16)
                    sp.dma_start(g_ea[0:EDIM, 0:r], eat[:, bass.ds(t * P, r)]).then_inc(g_load, 16)

                sp.dma_start(g_idx[0:P, :], src_col[0:P, :]).then_inc(g_load, 16)
                sp.dma_start(g_ea[0:EDIM, 0:P], eat[:, 0:P]).then_inc(g_load, 16)
                with sp.Fori(1, FULL) as t:
                    tile(t, P, t)
                tile(FULL, REST, FULL)

            for n, (b0, nb) in enumerate(BATCHES):
                sp.wait_ge(s_y[n], 1 + (shared(n) > 0))
                whole = nb if (b0 + nb) * P <= N else nb - 1
                sp.dma_start(out[b0 * P:(b0 + whole) * P, :].rearrange("(b p) h -> p b h", p=P),
                             y[:, b0:b0 + whole, :]).then_inc(s_out, 16)
                if whole < nb:
                    rows = N - (b0 + whole) * P
                    sp.dma_start(out[(b0 + whole) * P:N, :], y[0:rows, b0 + whole, :]).then_inc(s_out, 16)
            sp.wait_ge(s_out, 16 * (len(BATCHES) + (N % P > 0)))

        @block.gpsimd
        def _(pool):
            pool.memset(ident[:, :], 0.0).then_inc(s_const, 1)
            pool.iota(iota_i[:, :], pattern=[[1, WIN]], base=0, channel_multiplier=0).then_inc(s_const, 1)
            pool.iota(node[:, :], pattern=[[P, NBLK]], base=0, channel_multiplier=1).then_inc(s_const, 1)
            pool.wait_ge(s_const, 3)
            pool.affine_select(out=ident[:, :], in_=ident[:, :], compare_op=ALU.not_equal, fill=1.0,
                               base=0, pattern=[[-1, P]], channel_multiplier=1).then_inc(s_const, 1)

            def gather(slot, j, rows, index, done):
                pool.indirect_dma_start(
                    out=xg[0:rows, slot, j, :], out_offset=None, in_=x,
                    in_offset=bass.IndirectOffsetOnAxis(ap=index, axis=0)).then_inc(done, 16)

            def iteration(i):
                for g in range(SLOTS):
                    h, at = divmod(g * GROUP, TILES)
                    if at == 0:
                        wait_apart(pool, s_idx[h], (i + 1) * 16)
                    if not isinstance(i, int) or i:
                        wait_apart(pool, s_pre, (i - 1) * SLOTS + g + 1)
                    for j in range(GROUP - special(i, g)):
                        gather(g, j, P, idxb[h][:, at + j:at + j + 1], s_xg[g])

            run(pool, iteration)
            pool.wait_ge(s_last, 16 * len(LAST))
            pool.wait_ge(s_pre, (ITERS - 1) * SLOTS + 1)
            for j, r in LAST:
                gather(0, j, r, idx_last[0:r, j:j + 1], s_xg[0])

            pool.wait_ge(s_flag, 1)
            general = pool.value_load(flag[0:1, 0:1], min_val=0, max_val=1)
            with pool.If(general > 0):
                pool.wait_ge(s_h2[0], EARLY)
                pool.iota(iota_all[:, 0:N].bitcast(i32), pattern=[[1, N]], base=0, channel_multiplier=0)\
                    .then_inc(g_const, 1)

                def tile(r, n):
                    wait_apart(pool, g_load, (n + 1) * 32)
                    pool.indirect_dma_start(
                        out=g_xg[0:r, :], out_offset=None, in_=x,
                        in_offset=bass.IndirectOffsetOnAxis(ap=g_idx[0:r, :], axis=0)).then_inc(g_gat, 16)

                with pool.Fori(0, FULL) as t:
                    tile(P, t)
                tile(REST, FULL)

            pool.wait_ge(s_bn, 2)
            for n in range(BY_ACT, len(BATCHES)):
                b0, nb = BATCHES[n]
                a, b = b0 * P, min(N, (b0 + nb) * P)
                pool.tensor_scalar(accT[:, a:b], h2[:, a:b], bn_scale, bn_shift, ALU.mult, ALU.add)\
                    .then_inc(s_lift, 1)
                pool.wait_ge(s_lift, n - BY_ACT + 1)
                pool.tensor_scalar_max(accT[:, a:b], accT[:, a:b], 0.0).then_inc(s_relu[1], 1)

        @block.scalar
        def _(act):
            act.wait_ge(s_pro, 1)
            act.activation(epsc[:, 1:2], epsc[:, 0:1], ACT.Sqrt)
            act.dma_start(wea[0:EDIM, :], we).then_inc(s_we, 16)
            act.dma_start(wea[EDIM:K, :], be).then_inc(s_we, 16)
            act.dma_start(eps1, eps.partition_broadcast(P)).then_inc(s_we, 16)
            act.dma_start(xT[:, :], xt).then_inc(s_xt, 16)
            for j, v in enumerate((b1, b2, gamma, beta)):
                act.dma_start(par[:, j:j + 1], v).then_inc(s_small, 16)
            act.dma_start(w1s[:, :], w1).then_inc(s_small, 16)
            act.dma_start(w2s[:, :], w2).then_inc(s_small, 16)
            whole = N // P
            act.wait_ge(s_pro, 2)
            act.dma_start(xrow[:, 0:whole, :], x[0:whole * P, :].rearrange("(b p) h -> p b h", p=P))\
               .then_inc(s_xrow, 16)
            act.dma_start(xrow[0:N - whole * P, whole, :], x[whole * P:N, :]).then_inc(s_xrow, 16)
            act.wait_ge(s_xt, 16)
            act.wait_ge(s_pro, 3)
            act.activation(accT[:, 0:N], xT[:, :], ACT.Copy, scale=eps_plus1).then_inc(s_init, 1)
            act.activation(xT[:, :], xT[:, :], ACT.Copy, scale=2.0).then_inc(s_x2, 1)

            def hidden(c, z):
                act.wait_ge(s_m1[z], c + 1)
                if c >= 2:
                    act.wait_ge(s_m2[z], c - 1)
                w = CHUNKS[c][1]
                act.activation(h1[:, c % 2, 0:w], ps[:, bank1(c), 0:w], ACT.Relu, bias=b1s).then_inc(s_h1[z], 1)

            def second(c, z):
                act.wait_ge(s_m2[z], c + 1)
                c0, w = CHUNKS[c]
                act.activation(h2[:, c0:c0 + w], ps[:, bank2(c), 0:w], ACT.Identity, bias=b2s)\
                   .then_inc(s_h2[z], 1)

            def part(q, which):
                if which:
                    act.wait_ge(s_rest[0], q + 1)
                else:
                    act.wait_ge(s_xrow, 32)
                a, b = PIECES[q][0], sum(PIECES[q])
                act.activation(x3[:, a:b, which, :], xrow[:, a:b, :], ACT.Copy).then_inc(s_part[which], 1)

            def iteration(i):
                first = isinstance(i, int) and i == 0
                for g in range(SLOTS):
                    n = i * SLOTS + g
                    if special(i, g):
                        act.wait_ge(s_got, span(i, g) * NQ + NQ)
                        act.activation(got[:, 0, :], ps[:, 7, 2 * HID:3 * HID], ACT.Copy).then_inc(s_lo, 1)
                    act.wait_ge(s_pre, n + 1)
                    act.activation(msg[:, g % 2, :, :], msg[:, g % 2, :, :], ACT.Relu).then_inc(s_msg, 1)
                    if isinstance(i, int) and i == START - 1 and g < 2 * NQ:
                        part(g // 2, g % 2)
                    for c in early(i, g):
                        if c == 0:
                            act.wait_ge(s_small, 16 * 6)
                        hidden(c, 0)
                        if c:
                            second(c - 1, 0)

            general, redo = run(act, iteration, lambda: flags(act))
            second(EARLY - 1, 0)
            act.wait_ge(s_pre, LASTG + 1)
            k = LASTG % 2
            act.activation(msg[:, k, 0:LASTT, :], msg[:, k, 0:LASTT, :], ACT.Relu).then_inc(s_msg, 1)
            act.activation(msg[0:REST, k, LASTT, :], msg[0:REST, k, LASTT, :], ACT.Relu).then_inc(s_msg, 1)

            with act.If(redo > 0):
                act.wait_ge(s_st, EARLY)
                for c in range(EARLY):
                    hidden(c, 1)
                    second(c, 1)
            for c in range(EARLY, len(CHUNKS)):
                hidden(c, 0)
                if c > EARLY:
                    second(c - 1, 0)
            second(len(CHUNKS) - 1, 0)
            act.wait_ge(s_bn, 1)
            act.activation(bn_sd, bn_var, ACT.Sqrt, bias=epsc[:, 0:1]).then_inc(s_sd, 1)
            act.wait_ge(s_bn, 2)

            def normed(n):
                b0, nb = BATCHES[n]
                a, b = b0 * P, min(N, (b0 + nb) * P)
                act.activation(accT[:, a:b], h2[:, a:b], ACT.Relu, scale=bn_scale, bias=bn_shift)\
                   .then_inc(s_relu[0], 1)

            def deviation(n):
                b0, nb = BATCHES[n]
                act.wait_ge(s_var, n + 1)
                act.activation(ln[:, DEV, b0:b0 + nb], ln[:, VAR, b0:b0 + nb], ACT.Sqrt, bias=epsc[:, 0:1],
                               scale=1.0 / HID).then_inc(s_lsd, 1)

            normed(0)
            normed(1)
            deviation(0)
            normed(2)
            for n, (b0, nb) in enumerate(BATCHES):
                if n + 3 < BY_ACT:
                    normed(n + 3)
                if n + 1 < len(BATCHES):
                    deviation(n + 1)
                act.wait_ge(s_shift, n + 1)
                for b in range(b0, b0 + nb - shared(n)):
                    r = min(P, N - b * P)
                    last = act.activation(y[0:r, b, :], zt(b, r), ACT.Identity,
                                          scale=ln[0:r, INV, b:b + 1], bias=ln[0:r, SHIFT, b:b + 1])
                last.then_inc(s_y[n], 1)

        @block.vector
        def _(dve):
            done = [0]

            def step(ins):
                done[0] += 1
                ins.then_inc(s_pro, 1)
                dve.wait_ge(s_pro, done[0])

            step(dve.memset(epsc[:, 0:1], EPS))
            step(dve.memset(xrow[:, NBLK - 1, :], 0.0))
            for h in range(2):
                dve.memset(ea[h][EDIM:K, :], 1.0)
            dve.wait_ge(s_we, 16 * 3)
            step(dve.tensor_scalar_add(eps_plus1, eps1, 1.0))
            dve.memset(accT[:, N:N + WIN], 0.0).then_inc(s_init, 1)
            dve.memset(ones[:, :], 1.0)
            dve.memset(lnst[:, NBLK - 1, :], 0.0)
            dve.memset(leastT[:, :], 0.0)
            dve.wait_ge(s_dst, 32)
            step(dve.memset(least[:, LASTG:GROUPS], float(N)))
            dve.tensor_copy(rel[0:REST, FULL:FULL + 1], dsti[0:REST, FULL:FULL + 1])
            step(dve.tensor_copy(rel[:, 0:FULL], dsti[:, 0:FULL]))
            dve.tensor_reduce(least[:, 0:LOOPED], rel[:, 0:LOOPED * GROUP].rearrange("p (g t) -> p g t", t=GROUP),
                              AX.X, ALU.min)
            if LASTT:
                step(dve.tensor_reduce(least[:, LASTG:GROUPS], rel[:, LOOPED * GROUP:FULL], AX.X, ALU.min))
            step(dve.tensor_tensor(least[0:REST, LASTG:GROUPS], least[0:REST, LASTG:GROUPS],
                                   rel[0:REST, FULL:FULL + 1], ALU.min))
            dve.nop().then_inc(s_tr, 1)
            dve.wait_ge(s_tr, 2)
            for b in range(GBLK):
                w = min(P, GROUPS - b * P)
                last = dve.tensor_reduce(leastT[0:w, b:b + 1], ps[0:w, b, 0:P], AX.X, ALU.min)
            step(last)
            dve.wait_ge(s_const, 4)
            for b in range(GBLK):
                last = dve.tensor_scalar(diag[:, b, :], ident[:, :], leastT[:, b:b + 1], None, ALU.mult)
            last.then_inc(s_tr, 1)
            dve.wait_ge(s_tr, 4)
            step(dve.tensor_copy(base[:, :], ps[:, 4, 0:GROUPS]))
            dve.tensor_copy(basei[:, :], base[:, :])
            dve.tensor_copy(iota, iota_i[:, :])
            dve.tensor_copy(nodes, node[:, :])
            v = rel[:, 0:LOOPED * GROUP].rearrange("p (g t) -> p g t", t=GROUP)
            dve.tensor_tensor(v, v, base[:, 0:LOOPED].unsqueeze(2).to_broadcast([P, LOOPED, GROUP]), ALU.subtract)
            if LASTT:
                dve.tensor_scalar(rel[:, LOOPED * GROUP:FULL], rel[:, LOOPED * GROUP:FULL],
                                  base[:, LASTG:GROUPS], None, ALU.subtract)
            step(dve.tensor_scalar(rel[0:REST, FULL:FULL + 1], rel[0:REST, FULL:FULL + 1],
                                   base[0:REST, LASTG:GROUPS], None, ALU.subtract))
            step(dve.tensor_reduce(over[:, 0:1], rel[:, 0:FULL], AX.X, ALU.max))
            step(dve.tensor_tensor(over[0:REST, 0:1], over[0:REST, 0:1], rel[0:REST, FULL:FULL + 1], ALU.max))
            dve.nop().then_inc(s_tr, 1)
            dve.wait_ge(s_tr, 6)
            step(dve.tensor_reduce(overT[0:1, 0:1], ps[0:1, 5, 0:P], AX.X, ALU.max))
            step(dve.tensor_scalar(flagf[0:1, 0:1], overT[0:1, 0:1], float(WIN), None, ALU.is_ge))
            dve.tensor_copy(flag[0:1, 0:1], flagf[0:1, 0:1]).then_inc(s_flag, 1)
            step(dve.tensor_reduce(flagf[0:1, 1:2], base[0:1, LATE:GROUPS], AX.X, ALU.min))
            step(dve.tensor_scalar(flagf[0:1, 2:3], flagf[0:1, 1:2], float(EARLY_N), None, ALU.is_lt))
            step(dve.tensor_tensor(flagf[0:1, 3:4], flagf[0:1, 2:3], flagf[0:1, 0:1], ALU.max))
            dve.tensor_copy(flag[0:1, 1:2], flagf[0:1, 3:4]).then_inc(s_flag, 1)
            dve.nop().then_inc(s_tr, 1)

            def one_hot(n, k, first):
                if not first:
                    dve.wait_ge(s_win, n - 1)
                t0 = n * GROUP
                dve.tensor_tensor(
                    hot[:, k, :, :],
                    rel[:, bass.ds(t0, GROUP)].unsqueeze(2).to_broadcast([P, GROUP, WIN]),
                    iota.unsqueeze(1).to_broadcast([P, GROUP, WIN]), ALU.is_equal).then_inc(s_hot, 1)

            def add_x(i, g, n, first):
                dve.wait_ge(s_lin, n + 1)
                dve.wait_ge(s_xg[g], gathered(i, g))
                G = GROUP - special(i, g)
                last = dve.tensor_tensor(msg[:, g % 2, 0:G, :], ps_lin(g % 2)[:, 0:G, :], xg[:, g, 0:G, :], ALU.add)
                if G < GROUP:
                    k = span(i, g)
                    dve.wait_ge(s_lo, k + 1)
                    dve.tensor_tensor(got[:, 1, :], ps[:, 7, HID:2 * HID], got[:, 0, :], ALU.add).then_inc(s_join, 1)
                    dve.wait_ge(s_join, k * 2 + 1)
                    dve.tensor_tensor(got[:, 2, :], ps[:, 7, 0:HID], got[:, 1, :], ALU.add).then_inc(s_join, 1)
                    dve.wait_ge(s_join, k * 2 + 2)
                    last = dve.tensor_tensor(msg[:, g % 2, G, :], ps_lin(g % 2)[:, G, :], got[:, 2, :], ALU.add)
                last.then_inc(s_pre, 1)

            def select(i, g):
                q = g % SPAN
                if q >= NQ or not spans(i):
                    return
                h = g // SPAN
                at = span(i, g) * NQ + q
                if q == 0:
                    dve.wait_ge(s_srcb[h], (i - START) * 16 + 16)
                if not isinstance(at, int) or at >= 2:
                    dve.wait_ge(s_got, at - 1)
                b0, nb = PIECES[q]
                dve.tensor_tensor(sel[:, q % 2, 0:nb, :], srcb[h][:, :].unsqueeze(1).to_broadcast([P, nb, P]),
                                  nodes[:, b0:b0 + nb].unsqueeze(2).to_broadcast([P, nb, P]), ALU.is_equal)\
                   .then_inc(s_sel, 1)

            def remains(q, which):
                a, b = PIECES[q][0], sum(PIECES[q])
                dve.wait_ge(s_part[which], q + 1)
                to = xrow[:, a:b, :] if which == 0 else x3[:, a:b, 2, :]
                dve.tensor_tensor(to, xrow[:, a:b, :], x3[:, a:b, which, :], ALU.subtract)\
                   .then_inc(s_rest[which], 1)

            def add_window(n, k, first=False):
                at = dve.value_load(basei[0:1, bass.ds(n, 1)], min_val=0, max_val=N - 1)
                dve.wait_ge(s_win, n + 1)
                if not first:
                    dve.wait_ge(s_acc, n)
                dve.tensor_tensor(accT[:, bass.ds(at, WIN)], accT[:, bass.ds(at, WIN)], ps_win(k), ALU.add)\
                   .then_inc(s_acc, 1)

            def iteration(i):
                first = isinstance(i, int) and i == 0
                for g in range(SLOTS):
                    n = i * SLOTS + g
                    one_hot(n, g % 2, first and g < 2)
                    if g + 1 < SLOTS:
                        select(i, g + 1)
                    else:
                        select(i + 1, 0)
                    add_x(i, g, n, first and g < 2)
                    if not first or g >= 2:
                        if first and g == 2:
                            dve.wait_ge(s_init, 2)
                        for c in early(i, g):
                            dve.wait_ge(s_m1[0], c + 1)
                        add_window(n - 2, g % 2, first and g == 2)
                    if isinstance(i, int) and i == START - 1:
                        if g % 2 == 0 and g < 2 * NQ:
                            remains(g // 2, 0)
                        if g % 2 and g >= 3:
                            remains((g - 3) // 2, 1)
                    for c in early(i, g):
                        if c >= 2:
                            stats(c - 2, 0)

            def stats(c, z):
                c0, w = CHUNKS[c]
                dve.wait_ge(s_h2[z], c + 1)
                dve.bn_stats(bnst[:, c, :], h2[:, c0:c0 + w]).then_inc(s_st, 1)

            general, redo = run(dve, iteration, lambda: flags(dve))
            n, k = LASTG, LASTG % 2
            dve.wait_ge(s_win, n - 1)
            for j, r in LAST:
                last = dve.tensor_scalar(hot[0:r, k, j, :], iota[0:r, :], rel[0:r, LOOPED * GROUP + j:LOOPED * GROUP + j + 1],
                                         None, ALU.is_equal)
            last.then_inc(s_hot, 1)
            dve.wait_ge(s_lin, n + 1)
            dve.wait_ge(s_xg[0], gathered(ITERS - 1, 0) + 16 * len(LAST))
            for j, r in LAST:
                last = dve.tensor_tensor(msg[0:r, k, j, :], ps_lin(k)[0:r, j, :], xg[0:r, 0, j, :], ALU.add)
            last.then_inc(s_pre, 1)
            add_window(n - 2, k)
            add_window(n - 1, 1 - k)
            add_window(n, k)
            stats(EARLY - 2, 0)
            stats(EARLY - 1, 0)

            with dve.If(general > 0):
                dve.wait_ge(s_acc, GROUPS)
                dve.memset(g_ea[EDIM:K, :], 1.0).then_inc(g_const, 1)
                dve.wait_ge(g_const, 2)
                dve.tensor_copy(iota_all[:, 0:N], iota_all[:, 0:N].bitcast(i32)).then_inc(g_const, 1)
                dve.wait_ge(g_const, 3)
                STEPS = 8

                def tile(t, g, r, n):
                    def wait(k):
                        dve.wait_ge(g_vec, n * STEPS + k)
                    dve.tensor_scalar(g_dst[0:r, 0:1], rel[0:r, bass.ds(t, 1)], float(WIN), None, ALU.is_ge)\
                       .then_inc(g_vec, 1)
                    dve.tensor_scalar(g_dst[0:r, 1:2], rel[0:r, bass.ds(t, 1)], base[0:r, bass.ds(g, 1)], 1.0,
                                      ALU.add, ALU.add).then_inc(g_vec, 1)
                    wait(2)
                    dve.tensor_tensor(g_dst[0:r, 2:3], g_dst[0:r, 0:1], g_dst[0:r, 1:2], ALU.mult).then_inc(g_vec, 1)
                    wait(3)
                    dve.tensor_scalar_add(g_dst[0:r, 3:4], g_dst[0:r, 2:3], -1.0).then_inc(g_vec, 1)
                    wait(4)
                    dve.tensor_scalar(hot_all[0:r, :], iota_all[0:r, 0:N], g_dst[0:r, 3:4], None, ALU.is_equal)
                    dve.wait_ge(g_lin, n + 1)
                    dve.wait_ge(g_gat, (n + 1) * 16)
                    dve.tensor_tensor(g_msg[0:r, :], ps[0:r, 7, 0:HID], g_xg[0:r, :], ALU.add).then_inc(g_vec, 1)
                    wait(5)
                    dve.tensor_scalar_max(g_msg[0:r, :], g_msg[0:r, :], 0.0).then_inc(g_vec, 1)
                    for m, (a, b) in enumerate(SPLIT):
                        dve.wait_ge(g_sum, n * len(SPLIT) + m + 1)
                        c0, c1 = a * BANK, min(N, b * BANK)
                        dve.tensor_tensor(accT[:, c0:c1], accT[:, c0:c1],
                                          ps[:, 0:b - a, :].rearrange("p a n -> p (a n)")[:, 0:c1 - c0], ALU.add)\
                           .then_inc(g_vec, 1)
                    wait(STEPS)

                with dve.Fori(0, LOOPED) as g:
                    for j in range(GROUP):
                        tile(g * GROUP + j, g, P, g * GROUP + j)
                for j, r in LAST:
                    tile(LOOPED * GROUP + j, LASTG, r, LOOPED * GROUP + j)
            with dve.If(redo > 0):
                for c, (c0, w) in enumerate(CHUNKS[0:EARLY]):
                    dve.wait_ge(s_h2[1], c + 1)
                    last = dve.bn_stats(bnst[:, c, :], h2[:, c0:c0 + w])
                last.then_inc(s_redone, 1)
                dve.wait_ge(s_redone, 1)
            for c in range(EARLY, len(CHUNKS)):
                stats(c, 0)
            dve.wait_ge(s_st, len(CHUNKS))
            done[0] = len(CHUNKS)

            def stat(ins):
                done[0] += 1
                ins.then_inc(s_st, 1)
                dve.wait_ge(s_st, done[0])

            dve.bn_aggr(bn[:, 0:2], bnst[:, :, :].rearrange("p a b -> p (a b)")).then_inc(s_bn, 1)
            dve.wait_ge(s_bn, 1)
            dve.wait_ge(s_sd, 1)
            stat(dve.reciprocal(bn_inv, bn_sd))
            stat(dve.tensor_tensor(bn_scale, bn_inv, gms, ALU.mult))
            stat(dve.tensor_tensor(bn_prod, bn_scale, bn_mean, ALU.mult))
            dve.tensor_tensor(bn_shift, bts, bn_prod, ALU.subtract).then_inc(s_bn, 1)

            for n in range(len(BATCHES) + 1):
                if n < len(BATCHES):
                    b0, nb = BATCHES[n]
                    dve.wait_ge(s_zt, n + 1)
                    for b in range(b0, b0 + nb):
                        r = min(P, N - b * P)
                        last = dve.bn_stats(lnst[0:r, b, :], zt(b, r))
                    last.then_inc(s_stat, 1)
                if n:
                    c0, cb = BATCHES[n - 1]
                    dve.wait_ge(s_lsd, n)
                    dve.reciprocal(ln[:, INV, c0:c0 + cb], ln[:, DEV, c0:c0 + cb]).then_inc(s_inv, 1)
                if n < len(BATCHES):
                    dve.wait_ge(s_stat, 3 * n + 1)
                    me, qe, mo, qo = (lnst[:, b0:b0 + nb, j] for j in (1, 2, 4, 5))
                    m, v, u = (ln[:, j, b0:b0 + nb] for j in (MEAN2, VAR, TEMP))
                    dve.tensor_tensor(u, me, mo, ALU.subtract)
                    dve.tensor_tensor(m, me, mo, ALU.add)
                    dve.tensor_tensor(v, qe, qo, ALU.add).then_inc(s_stat, 1)
                if n:
                    dve.wait_ge(s_inv, n)
                    dve.scalar_tensor_tensor(out=ln[:, SHIFT, c0:c0 + cb], in0=ln[:, MEAN2, c0:c0 + cb],
                                             scalar=-0.5, in1=ln[:, INV, c0:c0 + cb], op0=ALU.mult, op1=ALU.mult)\
                       .then_inc(s_shift, 1)
                if n < len(BATCHES):
                    dve.wait_ge(s_stat, 3 * n + 2)
                    dve.scalar_tensor_tensor(out=u, in0=u, scalar=HID / 4.0, in1=u, op0=ALU.mult, op1=ALU.mult)\
                       .then_inc(s_stat, 1)
                    dve.wait_ge(s_stat, 3 * n + 3)
                    dve.tensor_tensor(v, v, u, ALU.add).then_inc(s_var, 1)
                if n and shared(n - 1):
                    dve.wait_ge(s_shift, n)
                    for b in range(c0 + cb - shared(n - 1), c0 + cb):
                        r = min(P, N - b * P)
                        last = dve.tensor_scalar(y[0:r, b, :], zt(b, r), ln[0:r, INV, b:b + 1], ln[0:r, SHIFT, b:b + 1],
                                                 ALU.mult, ALU.add)
                    last.then_inc(s_y[n - 1], 1)

        @block.tensor
        def _(pe):
            pe.wait_ge(s_const, 4)
            pe.wait_ge(s_tr, 1)
            for b in range(GBLK):
                w = min(P, GROUPS - b * P)
                last = pe.transpose(ps[0:w, b, 0:P], least[:, b * P:b * P + w], ident[:, :])
            last.then_inc(s_tr, 1)
            pe.wait_ge(s_tr, 3)
            for b in range(GBLK):
                w = min(P, GROUPS - b * P)
                last = pe.matmul(ps[:, 4, b * P:b * P + w], ones[:, :], diag[:, b, 0:w], start=True, stop=True)
            last.then_inc(s_tr, 1)
            pe.wait_ge(s_tr, 5)
            pe.transpose(ps[0:1, 5, 0:P], over[:, 0:1], ident[:, :]).then_inc(s_tr, 1)
            pe.wait_ge(s_we, 16 * 3)
            pe.wait_ge(s_tr, 7)

            def linear(h, at, k, tiles):
                for j, r in tiles:
                    last = pe.matmul(ps_lin(k)[0:r, j, :], ea[h][:, (at + j) * P:(at + j) * P + r], wea[:, :],
                                     start=True, stop=True)
                last.then_inc(s_lin, 1)

            def window(k, tiles):
                for j, r in tiles:
                    last = pe.matmul(ps_win(k), msg[0:r, k, j, :], hot[0:r, k, j, :],
                                     start=(j == 0), stop=(j == len(tiles) - 1))
                last.then_inc(s_win, 1)

            ALL = [(j, P) for j in range(GROUP)]

            def window_of(n, k, first):
                pe.wait_ge(s_msg, n + 1)
                pe.wait_ge(s_hot, n + 1)
                if not first:
                    pe.wait_ge(s_acc, n - 1)
                window(k, ALL)

            def gather(i, g, q):
                pe.wait_ge(s_sel, span(i, g) * NQ + (q + 1))
                if q == 0:
                    pe.wait_ge(s_rest[1], NQ)
                    pe.wait_ge(s_pre, i * SLOTS + g)
                b0, nb = PIECES[q]
                for b in range(nb):
                    last = pe.matmul(ps[:, 7, 0:3 * HID], sel[:, q % 2, b, :],
                                     x3[:, b0 + b, :, :].rearrange("p a h -> p (a h)"),
                                     start=(b0 + b == 0), stop=(b0 + b == NBLK - 1))
                last.then_inc(s_got, 1)

            def iteration(i):
                first = isinstance(i, int) and i == 0
                for g in range(SLOTS):
                    n = i * SLOTS + g
                    h, at = divmod(g * GROUP, TILES)
                    if at == 0:
                        pe.wait_ge(s_ea[h], (i + 1) * 16)
                    if not first or g >= 2:
                        pe.wait_ge(s_pre, n - 1)
                    linear(h, at, g % 2, ALL)
                    if spans(i) and g % SPAN < NQ:
                        gather(i, g, g % SPAN)
                    if not first or g >= 1:
                        window_of(n - 1, (g - 1) % 2, first and g < 3)
                    for c in early(i, g):
                        if c == 0:
                            pe.wait_ge(s_small, 16 * 6)
                        pe.wait_ge(s_acc, n - 2)
                        first_product(c, 0)
                        if c:
                            second_product(c - 1, 0)

            def first_product(c, z):
                c0, w = CHUNKS[c]
                if c:
                    pe.wait_ge(s_h1[z], min(c, EARLY))
                pe.matmul(ps[:, bank1(c), 0:w], w1s[:, :], accT[:, c0:c0 + w], start=True, stop=True)\
                  .then_inc(s_m1[z], 1)

            def second_product(c, z):
                w = CHUNKS[c][1]
                pe.wait_ge(s_h1[z], c + 1)
                if c:
                    pe.wait_ge(s_h2[z], min(c, EARLY))
                pe.matmul(ps[:, bank2(c), 0:w], w2s[:, :], h1[:, c % 2, 0:w], start=True, stop=True)\
                  .then_inc(s_m2[z], 1)

            general, redo = run(pe, iteration, lambda: flags(pe))
            pe.wait_ge(s_ea[0], (ITERS + 1) * 16)
            pe.wait_ge(s_pre, LASTG - 1)
            linear(0, 0, LASTG % 2, LAST)
            window_of(LASTG - 1, (LASTG - 1) % 2, False)
            second_product(EARLY - 1, 0)
            pe.wait_ge(s_msg, LASTG + 2)
            pe.wait_ge(s_hot, LASTG + 1)
            pe.wait_ge(s_acc, LASTG - 1)
            window(LASTG % 2, LAST)

            with pe.If(general > 0):
                pe.wait_ge(g_const, 3)
                pe.wait_ge(s_h2[0], EARLY)
                STEPS = 8

                def tile(r, n, first):
                    pe.wait_ge(g_load, (n + 1) * 32)
                    if not first:
                        pe.wait_ge(g_vec, n * STEPS)
                    pe.matmul(ps[0:r, 7, 0:HID], g_ea[:, 0:r], wea[:, :], start=True, stop=True).then_inc(g_lin, 1)
                    pe.wait_ge(g_vec, n * STEPS + 6)
                    for m, (a, b) in enumerate(SPLIT):
                        if m:
                            pe.wait_ge(g_vec, n * STEPS + 6 + m)
                        for q in range(a, b):
                            w = min(BANK, N - q * BANK)
                            last = pe.matmul(ps[:, q - a, 0:w], g_msg[0:r, :], hot_all[0:r, q * BANK:q * BANK + w],
                                             start=True, stop=True)
                        last.then_inc(g_sum, 1)

                tile(P, 0, True)
                with pe.Fori(1, FULL) as t:
                    tile(P, t, False)
                tile(REST, FULL, False)
                pe.wait_ge(g_vec, (FULL + 1) * STEPS)

            with pe.If(redo > 0):
                pe.wait_ge(s_acc, GROUPS)
                pe.wait_ge(s_h2[0], EARLY)
                for c in range(EARLY):
                    first_product(c, 1)
                    second_product(c, 1)
                pe.wait_ge(s_h2[1], EARLY)
            pe.wait_ge(s_acc, GROUPS)
            for c in range(EARLY, len(CHUNKS)):
                first_product(c, 0)
                if c > EARLY:
                    second_product(c - 1, 0)
            second_product(len(CHUNKS) - 1, 0)

            def rows(n, second):
                b0, nb = BATCHES[n]
                for b in range(b0, b0 + nb):
                    r = min(P, N - b * P)
                    of = accT if second else xT
                    last = pe.matmul(zt(b, r), of[:, b * P:b * P + r], ident[:, :], is_transpose=True,
                                     start=not second and b % 4 == 0,
                                     stop=second and (b % 4 == 3 or b == NBLK - 1))
                return last

            def x_rows(n):
                b0, nb = BATCHES[n]
                for m, (c0, cb) in enumerate(BATCHES):
                    if (c0 + cb - 1) // 4 >= b0 // 4 - 8 and c0 // 4 <= (b0 + nb - 1) // 4 - 8:
                        pe.wait_ge(s_y[m], 1 + (shared(m) > 0))
                rows(n, False)

            pe.wait_ge(s_x2, 1)
            for n in range(3):
                x_rows(n)
            pe.wait_ge(s_h2[0], len(CHUNKS))
            x_rows(3)
            for n in range(len(BATCHES)):
                if n < BY_ACT:
                    pe.wait_ge(s_relu[0], n + 1)
                else:
                    pe.wait_ge(s_relu[1], n - BY_ACT + 1)
                rows(n, True).then_inc(s_zt, 1)
                if 4 <= n + 1 < len(BATCHES):
                    x_rows(n + 1)


def kernel(**inputs):
    import numpy as _np
    import concourse.bacc as _bacc
    from concourse import mybir as _mybir
    from concourse.bass_utils import run_bass_kernel_spmd as _run

    P, TILES, PARTS = 128, 20, 2
    a = {k: _np.asarray(v) for k, v in inputs.items()}
    x, src, dst, ea = a["x"], a["src"], a["dst"], a["edge_attr_64"]
    E = src.shape[0]
    full = E // P
    spans = full // (PARTS * TILES) * PARTS
    col = lambda v: v.reshape(-1, 1)
    data = {
        "x": x,
        "xt": x.T,
        "src_loop": src[:spans * TILES * P].reshape(spans, TILES, P).transpose(0, 2, 1),
        "src_row": src.reshape(1, -1),
        "src_col": col(src),
        "dst_tiles": dst[:full * P].reshape(full, P).T,
        "dst_last": col(dst[full * P:]),
        "eat": ea.T,
        "we": a["L0_gnn_We"],
        "be": a["L0_gnn_be"].reshape(1, -1),
        "w1": a["L0_gnn_W1"],
        "b1": col(a["L0_gnn_b1"]),
        "w2": a["L0_gnn_W2"],
        "b2": col(a["L0_gnn_b2"]),
        "gamma": col(a["L0_gnn_gamma"]),
        "beta": col(a["L0_gnn_beta"]),
        "eps": a["L0_gnn_eps"].reshape(1, 1),
    }
    nc = _bacc.Bacc("TRN2", target_bir_lowering=False, num_devices=1)
    arrays, args = {}, []
    for name, v in data.items():
        v = _np.ascontiguousarray(v)
        arrays[f"in_{name}"] = v
        args.append(nc.dram_tensor(f"in_{name}", v.shape, _mybir.dt.from_np(v.dtype), kind="ExternalInput").ap())
    args.append(nc.dram_tensor("out", x.shape, _mybir.dt.float32, kind="ExternalOutput").ap())
    gine_layer_kernel(nc, *args)
    r = _run(nc, [arrays], core_ids=[0])
    return r.results[0]["out"]
```
